# Optimizing a Trainium2 kernel written in Bass

```python
import numpy as np
import jax
import jax.numpy as jnp

def _softmax(x, axis=-1):
    return jax.nn.softmax(x, axis=axis)

def _gelu(x):
    return jax.nn.gelu(x, approximate=True)

def _silu(x):
    return jax.nn.silu(x)

def _sigmoid(x):
    return jax.nn.sigmoid(x)

def _layernorm(x, axis=-1, eps=1e-05):
    m = jnp.mean(x, axis=axis, keepdims=True)
    v = jnp.var(x, axis=axis, keepdims=True)
    return (x - m) / jnp.sqrt(v + eps)

def _scatter_add(tgt, idx, src, axis=0):
    return tgt.at[idx].add(src)

def _segment_sum(src, seg, n):
    return jax.ops.segment_sum(src, seg, n)
kernel_name = 'mk_conv_preact_d4_conv_nchw2048_r4_3a6150'

def setup_inputs(seed: int=0):
    np.random.seed(seed)
    _w = jnp.asarray

    def _rec_inputs():
        import jax
        import jax.numpy as jnp
        _gk = jax.random.key(seed)
        x = -0.000125 + 0.9999 * jax.random.normal(jax.random.fold_in(_gk, 1), (4, 512, 16, 16), jnp.float32)
        return x
    x = _rec_inputs()

    def _L0_conv_setup():
        import jax, jax.numpy as jnp
        import numpy as np
        C = 512
        RED = 8
        D = C // RED
        key = jax.random.key(seed)
        ks = jax.random.split(key, 8)
        n, h, w = (4, 16, 16)
        x = jax.random.normal(ks[0], (n, C, h, w), dtype=jnp.float32)
        w1 = jax.random.normal(ks[1], (D, C), dtype=jnp.float32) * 0.02
        b1 = jnp.zeros((D,), dtype=jnp.float32)
        w2 = jax.random.normal(ks[2], (D, C), dtype=jnp.float32) * 0.02
        b2 = jnp.zeros((D,), dtype=jnp.float32)
        w3 = jax.random.normal(ks[3], (C, C), dtype=jnp.float32) * 0.02
        b3 = jnp.zeros((C,), dtype=jnp.float32)
        alpha = jnp.zeros((1,), dtype=jnp.float32)
        return {'x': x, 'w1': w1, 'b1': b1, 'w2': w2, 'b2': b2, 'w3': w3, 'b3': b3, 'alpha': alpha}
    _L0_conv_all = _L0_conv_setup()
    _L0_conv_in = {k: v for k, v in _L0_conv_all.items() if k in ('w1', 'b1', 'w2', 'b2', 'w3', 'b3', 'alpha')}
    del _L0_conv_all

    def _L1_conv_setup():
        import jax, jax.numpy as jnp
        import numpy as np
        key = jax.random.key(seed)
        k1, k2, k3 = jax.random.split(key, 3)
        N, C, H, W = (4, 512, 32, 48)
        feature = jax.random.normal(k1, (N, C, H, W), dtype=jnp.float32)
        conv_w = jax.random.normal(k2, (C, C, 1, 9), dtype=jnp.float32) * 0.01
        conv_b = jax.random.normal(k3, (C,), dtype=jnp.float32) * 0.01
        prelu_a = jnp.asarray(0.25, dtype=jnp.float32)
        return {'feature': feature, 'conv_w': conv_w, 'conv_b': conv_b, 'prelu_a': prelu_a}
    _L1_conv_all = _L1_conv_setup()
    _L1_conv_in = {k: v for k, v in _L1_conv_all.items() if k in ('conv_w', 'conv_b', 'prelu_a')}
    del _L1_conv_all

    def _L2_conv_setup():
        import jax, jax.numpy as jnp
        import numpy as np
        C = 512
        RED = 8
        D = C // RED
        key = jax.random.key(seed)
        ks = jax.random.split(key, 8)
        n, h, w = (4, 16, 16)
        x = jax.random.normal(ks[0], (n, C, h, w), dtype=jnp.float32)
        w1 = jax.random.normal(ks[1], (D, C), dtype=jnp.float32) * 0.02
        b1 = jnp.zeros((D,), dtype=jnp.float32)
        w2 = jax.random.normal(ks[2], (D, C), dtype=jnp.float32) * 0.02
        b2 = jnp.zeros((D,), dtype=jnp.float32)
        w3 = jax.random.normal(ks[3], (C, C), dtype=jnp.float32) * 0.02
        b3 = jnp.zeros((C,), dtype=jnp.float32)
        alpha = jnp.zeros((1,), dtype=jnp.float32)
        return {'x': x, 'w1': w1, 'b1': b1, 'w2': w2, 'b2': b2, 'w3': w3, 'b3': b3, 'alpha': alpha}
    _L2_conv_all = _L2_conv_setup()
    _L2_conv_in = {k: v for k, v in _L2_conv_all.items() if k in ('w1', 'b1', 'w2', 'b2', 'w3', 'b3', 'alpha')}
    del _L2_conv_all

    def _L3_conv_setup():
        import jax, jax.numpy as jnp
        import numpy as np
        N, C, H, WD = (4, 512, 48, 24)
        KH = 9
        key = jax.random.key(seed)
        k1, k2, k3 = jax.random.split(key, 3)
        fea = jax.random.normal(k1, (N, C, H, WD), dtype=jnp.float32)
        W = jax.random.normal(k2, (C, C, KH, 1), dtype=jnp.float32) * 0.01
        b = jax.random.normal(k3, (C,), dtype=jnp.float32) * 0.01
        return {'fea': fea, 'W': W, 'b': b}
    _L3_conv_all = _L3_conv_setup()
    _L3_conv_in = {k: v for k, v in _L3_conv_all.items() if k in ('W', 'b')}
    del _L3_conv_all
    return {'x': x, 'L0_conv_w1': _L0_conv_in['w1'], 'L0_conv_b1': _L0_conv_in['b1'], 'L0_conv_w2': _L0_conv_in['w2'], 'L0_conv_b2': _L0_conv_in['b2'], 'L0_conv_w3': _L0_conv_in['w3'], 'L0_conv_b3': _L0_conv_in['b3'], 'L0_conv_alpha': _L0_conv_in['alpha'], 'L1_conv_conv_w': _L1_conv_in['conv_w'], 'L1_conv_conv_b': _L1_conv_in['conv_b'], 'L1_conv_prelu_a': _L1_conv_in['prelu_a'], 'L2_conv_w1': _L2_conv_in['w1'], 'L2_conv_b1': _L2_conv_in['b1'], 'L2_conv_w2': _L2_conv_in['w2'], 'L2_conv_b2': _L2_conv_in['b2'], 'L2_conv_w3': _L2_conv_in['w3'], 'L2_conv_b3': _L2_conv_in['b3'], 'L2_conv_alpha': _L2_conv_in['alpha'], 'L3_conv_W': _L3_conv_in['W'], 'L3_conv_b': _L3_conv_in['b']}

def reference(x, L0_conv_w1, L0_conv_b1, L0_conv_w2, L0_conv_b2, L0_conv_w3, L0_conv_b3, L0_conv_alpha, L1_conv_conv_w, L1_conv_conv_b, L1_conv_prelu_a, L2_conv_w1, L2_conv_b1, L2_conv_w2, L2_conv_b2, L2_conv_w3, L2_conv_b3, L2_conv_alpha, L3_conv_W, L3_conv_b):
    import jax
    import jax.numpy as jnp

    def _L0_conv_ref(x, w1, b1, w2, b2, w3, b3, alpha):
        import jax, jax.numpy as jnp
        import numpy as np
        C = 512
        RED = 8
        D = C // RED
        n, c, h, w = x.shape
        hw = h * w
        xf = x.reshape(n, c, hw)
        e1 = jax.nn.relu(jnp.einsum('dc,ncp->ndp', w1, xf) + b1[None, :, None])
        e2 = jax.nn.relu(jnp.einsum('dc,ncp->ndp', w2, xf) + b2[None, :, None])
        assembly = jax.nn.relu(jnp.einsum('oc,ncp->nop', w3, xf) + b3[None, :, None])
        scores = jnp.einsum('ndi,ndj->nij', e1, e2)
        attn = jax.nn.softmax(scores, axis=-1)
        out = jnp.einsum('ncj,nij->nci', xf, attn)
        y = alpha[0] * out + assembly
        return y.reshape(n, c, h, w)

    def _L1_conv_ref(feature, conv_w, conv_b, prelu_a):
        import jax, jax.numpy as jnp
        import numpy as np
        Wc = conv_w[:, :, 0, 4]

        def step(prev, x_i):
            y = jnp.einsum('oc,nch->noh', Wc, prev) + conv_b[None, :, None]
            y = jnp.where(y >= 0, y, prelu_a * y)
            cur = y + x_i
            return (cur, cur)
        x = jnp.moveaxis(feature, 3, 0)
        _, fwd_rest = jax.lax.scan(step, x[0], x[1:])
        fl = jnp.concatenate([x[0:1], fwd_rest], axis=0)
        _, bwd_rest = jax.lax.scan(step, fl[-1], fl[:-1], reverse=True)
        out = jnp.concatenate([bwd_rest, fl[-1:]], axis=0)
        return jnp.moveaxis(out, 0, 3)

    def _L2_conv_ref(x, w1, b1, w2, b2, w3, b3, alpha):
        import jax, jax.numpy as jnp
        import numpy as np
        C = 512
        RED = 8
        D = C // RED
        n, c, h, w = x.shape
        hw = h * w
        xf = x.reshape(n, c, hw)
        e1 = jax.nn.relu(jnp.einsum('dc,ncp->ndp', w1, xf) + b1[None, :, None])
        e2 = jax.nn.relu(jnp.einsum('dc,ncp->ndp', w2, xf) + b2[None, :, None])
        assembly = jax.nn.relu(jnp.einsum('oc,ncp->nop', w3, xf) + b3[None, :, None])
        scores = jnp.einsum('ndi,ndj->nij', e1, e2)
        attn = jax.nn.softmax(scores, axis=-1)
        out = jnp.einsum('ncj,nij->nci', xf, attn)
        y = alpha[0] * out + assembly
        return y.reshape(n, c, h, w)

    def _L3_conv_ref(fea, W, b):
        import jax, jax.numpy as jnp
        import numpy as np
        N, C, H, WD = (4, 512, 48, 24)
        KH = 9
        kh = W.shape[2]
        Wm = W[:, :, (kh - 1) // 2, 0]
        bb = b[None, :, None]

        def step(carry, x):
            new = jax.nn.relu(jnp.einsum('oc,ncw->now', Wm, carry) + bb) + x
            return (new, new)
        xs = jnp.moveaxis(fea, 2, 0)
        _, ys = jax.lax.scan(step, xs[0], xs[1:])
        down = jnp.concatenate([xs[:1], ys], axis=0)
        _, ys2 = jax.lax.scan(step, down[-1], down[:-1], reverse=True)
        stack = jnp.concatenate([ys2, down[-1:]], axis=0)
        return jnp.moveaxis(stack, 0, 2)

    def _gn(v, G=32, eps=1e-05):
        B_, C_, H_, W_ = v.shape
        g = v.reshape(B_, G, C_ // G, H_, W_)
        m = jnp.mean(g, axis=(2, 3, 4), keepdims=True)
        s = jnp.var(g, axis=(2, 3, 4), keepdims=True)
        return ((g - m) / jnp.sqrt(s + eps)).reshape(v.shape)

    def _ln_c(v, eps=1e-06):
        m = jnp.mean(v, axis=1, keepdims=True)
        s = jnp.var(v, axis=1, keepdims=True)
        return (v - m) / jnp.sqrt(s + eps)

    def _ln_t(v, eps=1e-05):
        m = jnp.mean(v, axis=-1, keepdims=True)
        s = jnp.var(v, axis=-1, keepdims=True)
        return (v - m) / jnp.sqrt(s + eps)

    def _to_tokens(v):
        B_, C_, H_, W_ = v.shape
        return v.reshape(B_, C_, H_ * W_).transpose(0, 2, 1)

    def _from_tokens(t, like):
        B_, C_, H_, W_ = like.shape
        return t.transpose(0, 2, 1).reshape(B_, C_, H_, W_)
    x = x + _L0_conv_ref(_gn(x), L0_conv_w1, L0_conv_b1, L0_conv_w2, L0_conv_b2, L0_conv_w3, L0_conv_b3, L0_conv_alpha)
    x = x + _L1_conv_ref(_gn(x), L1_conv_conv_w, L1_conv_conv_b, L1_conv_prelu_a)
    x = x + _L2_conv_ref(_gn(x), L2_conv_w1, L2_conv_b1, L2_conv_w2, L2_conv_b2, L2_conv_w3, L2_conv_b3, L2_conv_alpha)
    x = x + _L3_conv_ref(_gn(x), L3_conv_W, L3_conv_b)
    return x

_drawn_inputs = setup_inputs


def setup_inputs(seed=0):
    import zlib

    import numpy as np

    out = dict(_drawn_inputs(seed))
    spreads = {'L0_conv_b1': (0.0, 0.1),
     'L0_conv_b2': (0.0, 0.1),
     'L0_conv_b3': (0.0, 0.1),
     'L2_conv_b1': (0.0, 0.1),
     'L2_conv_b2': (0.0, 0.1),
     'L2_conv_b3': (0.0, 0.1)}
    factors = {'L1_conv_conv_b': 8.0, 'L3_conv_b': 8.0}
    for name, (base, spread) in spreads.items():
        noise = np.random.default_rng([zlib.crc32(name.encode()), seed]).standard_normal(out[name].shape)
        drawn = base * np.exp(spread * noise) if base else spread * noise
        out[name] = jnp.asarray(drawn.astype(out[name].dtype))
    for name, factor in factors.items():
        out[name] = (out[name] * factor).astype(out[name].dtype)
    return out
```

```python
from contextlib import ExitStack

import concourse.bass as bass
from concourse import mybir
from concourse.alu_op_type import AluOpType as ALU

F32 = mybir.dt.float32
ACT = mybir.ActivationFunctionType
AX_X = mybir.AxisListType.X

P = 128
N = 4
C = 512
K = C // P
T = 16
POS = T * T
PC = POS // P
D = C // 8
G = 32
CG = C // G
COLS = N * T
NC = K * N
EPS = 1e-5

B12_0, B3_0, AL_0, CB_1, PA_1, B12_2, B3_2, AL_2, CB_3, NPAR = 0, 1, 5, 6, 10, 11, 12, 16, 17, 21

ORDER = {1: [(0, 0), (0, 1), (1, 0), (1, 1), (0, 2), (1, 2), (2, 0), (3, 0),
             (2, 1), (3, 1), (0, 3), (1, 3), (2, 2), (3, 2), (2, 3), (3, 3)],
         3: [(0, 0), (0, 1), (1, 0), (1, 1), (2, 0), (0, 2), (2, 1), (3, 0),
             (3, 1), (1, 2), (2, 2), (3, 2), (0, 3), (1, 3), (2, 3), (3, 3)]}
UNIT = {1: 2, 3: 1}


class NormSems:

    def __init__(self, sem, l):
        self.stats = sem(f"stats_ready{l}")
        self.mean = sem(f"mean_summed{l}")
        self.vadd = sem(f"vadd_ready{l}")
        self.var = sem(f"var_summed{l}")
        self.gvar = sem(f"gvar_ready{l}")
        self.rstd = sem(f"rstd_ready{l}")
        self.done = sem(f"norm_ready{l}")


class AttentionSems:

    def __init__(self, sem, l):
        self.xn_ready = sem(f"xn_ready{l}")
        self.xnT_mm = sem(f"xnT_mm{l}")
        self.xnT_copied = sem(f"xnT_copied{l}")
        self.e_mm = sem(f"e_mm{l}")
        self.e_ready = sem(f"e_ready{l}")
        self.a_mm = sem(f"a_mm{l}")
        self.r_ready = sem(f"r_ready{l}")
        self.s_mm = sem(f"s_mm{l}")
        self.nmx_ready = sem(f"nmx_ready{l}")
        self.exp_done = sem(f"exp_done{l}")
        self.p_ready = sem(f"p_ready{l}")
        self.pt_mm = sem(f"pt_mm{l}")
        self.pt_copied = sem(f"pt_copied{l}")
        self.o_mm = sem(f"o_mm{l}")
        self.u_done = sem(f"u_done{l}")
        self.x_done = sem(f"x_done{l}")
        self.chain = sem(f"softmax_chain{l}")


class ScanSems:

    def __init__(self, sem, l):
        units = range(K // UNIT[l])
        self.first = sem(f"first_state{l}")
        self.bias = sem(f"input_bias{l}")
        self.inb = [sem(f"inputs_ready{l}_{n}") for n in range(N)]
        self.y = [sem(f"products_done{l}_{u}") for u in units]
        self.parts = sem(f"low_lin_ready{l}")
        self.state = [sem(f"state_ready{l}_{u}") for u in units]
        self.sb = sem(f"state_bias_ready{l}")
        self.x = sem(f"x_updated{l}")


def preact_stack(nc, a):
    with ExitStack() as ctx:
        def sb(name, shape):
            return ctx.enter_context(nc.sbuf_tensor(name, shape, F32))

        def sem(name):
            return ctx.enter_context(nc.semaphore(name))

        bank = [ctx.enter_context(nc.psum_tensor(f"bank{b}", [P, 512], F32)) for b in range(8)]

        x0 = sb("x0", [P, N, K, POS])
        par = sb("par", [P, NPAR])
        ident = sb("ident", [P, P])
        gavg = sb("gavg", [P, P])
        w12 = {l: sb(f"w12_{l}", [P, K, 2 * D]) for l in (0, 2)}
        w3 = {l: sb(f"w3_{l}", [P, K, C]) for l in (0, 2)}
        wc = {l: sb(f"wc_{l}", [P, K, C]) for l in (1, 3)}

        xw = sb("xw", [P, T, K, COLS])
        xh = sb("xh", [P, T, K, COLS])

        st = sb("st", [P, NC, 2, 3])
        dev = sb("dev", [P, NC, 2])
        dev2 = sb("dev2", [P, NC, 2])
        vadd = sb("vadd", [P, NC, 2])
        gmean = sb("gmean", [P, NC])
        gvar = sb("gvar", [P, NC])
        mhalf = sb("mhalf", [P, NC])
        rstd = sb("rstd", [P, NC])
        nmr = sb("nmr", [P, NC])

        xn = [sb(f"xn{s}", [P, K, POS]) for s in range(2)]
        xnT = sb("xnT", [P, PC, C])
        e1 = sb("e1", [D, POS])
        e2 = sb("e2", [D, POS])
        prob = sb("prob", [P, PC, POS])
        probT = sb("probT", [P, PC, POS])
        mx = sb("mx", [P, PC])
        nmx = sb("nmx", [P, PC])
        rsum = sb("rsum", [P, PC])
        rrec = sb("rrec", [P, PC])
        rel = sb("rel", [P, K, POS])
        upd = sb("upd", [P, K, POS])

        state = sb("state", [P, T, K, COLS])
        inb = sb("inb", [P, T, K, COLS])
        low = sb("low", [P, K, COLS])
        lin = sb("lin", [P, K, COLS])
        negb = sb("negb", [P, K])
        bnmr = sb("bnmr", [P, NC])
        oma = sb("oma", [P, 1])

        s_x = [sem(f"x_loaded{n}") for n in range(N)]
        s_small = sem("small_loaded")
        s_w12 = {l: sem(f"w12_loaded{l}") for l in (0, 2)}
        s_w3 = {l: sem(f"w3_loaded{l}") for l in (0, 2)}
        s_wc = {l: sem(f"wc_loaded{l}") for l in (1, 3)}
        s_mhalf = sem("mhalf_set")
        s_out = sem("out_stored")

        norm = [NormSems(sem, l) for l in range(4)]
        att = {l: AttentionSems(sem, l) for l in (0, 2)}
        scan = {l: ScanSems(sem, l) for l in (1, 3)}
        s_dve = sem("vector_chain")

        def image_in(l, n):
            if l == 0:
                return x0[:, n]
            return xw.rearrange("p w k (n h) -> p n k h w", n=N)[:, n]

        def image_out(l, n):
            dst = xw if l == 0 else xh
            return dst.rearrange("p t k (n j) -> p n k t j", n=N)[:, n]

        block = ctx.enter_context(nc.Block())

        @block.sync
        def _(sp):
            sp.dma_start(par[:], a["par"]).then_inc(s_small, 16)
            sp.dma_start(gavg[:], a["gavg"]).then_inc(s_small, 16)
            sp.dma_start(ident[:], a["ident"]).then_inc(s_small, 16)
            for n in range(N):
                sp.dma_start(x0[:, n], a["x"][:, n]).then_inc(s_x[n], 16)
            sp.dma_start(wc[1][:], a["wc1"]).then_inc(s_wc[1], 16)
            sp.dma_start(wc[3][:], a["wc3"]).then_inc(s_wc[3], 16)
            with sp.Fori(0, T) as i:
                t = i * -1 + (T - 1)
                sp.wait_ge(scan[3].x, i + 1)
                sp.dma_start(a["out"][:, t], xh[:, t]).then_inc(s_out, 16)
            sp.wait_ge(s_out, 16 * T)

        @block.tensor
        def _(pe):
            def group_norm(l):
                s = norm[l]
                pe.wait_ge(s.stats, NC)
                if l == 0:
                    pe.wait_ge(s_small, 48)
                nc.tensor.matmul(bank[4][:, 0:NC], gavg[:], st[:, :, 0, 1], start=True, stop=False)
                nc.tensor.matmul(bank[4][:, 0:NC], gavg[:], st[:, :, 1, 1], start=False, stop=True)\
                    .then_inc(s.mean, 1)
                pe.wait_ge(s.vadd, 1)
                nc.tensor.matmul(bank[5][:, 0:NC], gavg[:], vadd[:, :, 0], start=True, stop=False)
                nc.tensor.matmul(bank[5][:, 0:NC], gavg[:], vadd[:, :, 1], start=False, stop=True)\
                    .then_inc(s.var, 1)

            def attention(l):
                s = att[l]
                pe.wait_ge(s_w12[l], 16)
                pe.wait_ge(s_w3[l], 16)

                def relu_branch(xn_s, m, done):
                    for k in range(K):
                        mm = nc.tensor.matmul(bank[2 + m // 2][:, m % 2 * POS:(m % 2 + 1) * POS],
                                              w3[l][:, k, m * P:(m + 1) * P], xn_s[:, k],
                                              start=(k == 0), stop=(k == K - 1))
                    if done:
                        mm.then_inc(s.a_mm, 1)

                with pe.Fori(0, N // 2) as pair:
                    for h in range(2):
                        n = pair * 2 + h
                        pe.wait_ge(s.xn_ready, (n + 1) * K)
                        for pc in range(PC):
                            for k in range(K):
                                mm = nc.tensor.transpose(bank[6 + pc][:, k * P:(k + 1) * P],
                                                         xn[h][:, k, pc * P:(pc + 1) * P], ident[:])
                            mm.then_inc(s.xnT_mm, 1)
                        for k in range(K):
                            mm = nc.tensor.matmul(bank[1][:, 0:POS], w12[l][:, k], xn[h][:, k],
                                                  start=(k == 0), stop=(k == K - 1))
                        mm.then_inc(s.e_mm, 1)
                        relu_branch(xn[h], 0, False)
                        pe.wait_ge(s.e_ready, (n + 1) * 2)
                        for ic in range(PC):
                            mm = nc.tensor.matmul(bank[0][:, ic * POS:(ic + 1) * POS],
                                                  e1[:, ic * P:(ic + 1) * P], e2[:], start=True, stop=True)
                        mm.then_inc(s.s_mm, 1)
                        relu_branch(xn[h], 1, True)
                        relu_branch(xn[h], 2, False)
                        pe.wait_ge(s.p_ready, (n + 1) * PC)
                        for jc in range(PC):
                            for ic in range(PC):
                                mm = nc.tensor.transpose(bank[1 - jc][:, ic * P:(ic + 1) * P],
                                                         prob[:, ic, jc * P:(jc + 1) * P], ident[:])
                            mm.then_inc(s.pt_mm, 1)
                        relu_branch(xn[h], 3, True)
                        pe.wait_ge(s.xnT_copied, (n + 1) * PC)
                        pe.wait_ge(s.pt_copied, (n + 1) * PC)
                        for m in range(K):
                            for jc in range(PC):
                                mm = nc.tensor.matmul(bank[4 + m // 2][:, m % 2 * POS:(m % 2 + 1) * POS],
                                                      xnT[:, jc, m * P:(m + 1) * P], probT[:, jc],
                                                      start=(jc == 0), stop=(jc == PC - 1))
                            if m % 2:
                                mm.then_inc(s.o_mm, 1)
                            if m == 1:
                                pe.wait_ge(s.r_ready, (n + 1) * K)

            def scan_layer(l):
                s = scan[l]
                pe.wait_ge(s_wc[l], 16)

                size = UNIT[l]

                def step(q, src, parity):
                    seen = set()
                    for j, (k, m) in enumerate(ORDER[l]):
                        u = k // size
                        if u not in seen and isinstance(q, int) and q == 0:
                            pe.wait_ge(s.first, 1)
                        elif u not in seen:
                            pe.wait_ge(s.state[u], q)
                        seen.add(u)
                        clear = all(o[1] // size != m // size for o in ORDER[l][:j])
                        final = all(o[1] // size != m // size for o in ORDER[l][j + 1:])
                        mm = nc.tensor.matmul(
                            bank[(K // size) * parity + m // size][:, m % size * COLS:(m % size + 1) * COLS],
                            wc[l][:, k, m * P:(m + 1) * P], src[:, k],
                            start=clear, stop=final, skip_group_check=True)
                        if final:
                            mm.then_inc(s.y[m // size], 1)

                step(0, state[:, 0], 0)
                with pe.Fori(0, (T - 2) // 2) as i:
                    for h in range(2):
                        step(i * 2 + 1 + h, state[:, i * 2 + 1 + h], (1 + h) % 2)
                step(T - 1, state[:, T - 1], 1)
                with pe.Fori(0, (T - 2) // 2) as i:
                    last = i * -2 + (T - 2)
                    for h in range(2):
                        step(i * 2 + T + h, state[:, last + -h], h % 2)

            group_norm(0)
            attention(0)
            group_norm(1)
            scan_layer(1)
            group_norm(2)
            attention(2)
            group_norm(3)
            scan_layer(3)

        @block.scalar
        def _(act):
            for l in (0, 2):
                act.dma_start(w12[l][:], a[f"w12_{l}"]).then_inc(s_w12[l], 16)
                act.dma_start(w3[l][:], a[f"w3_{l}"]).then_inc(s_w3[l], 16)

            def attention(l, b12, b3):
                s = att[l]
                with act.Fori(0, N // 2) as pair:
                    for h in range(2):
                        n = pair * 2 + h
                        act.wait_ge(s.xnT_mm, n * PC + 1)
                        nc.scalar.copy(xnT[:, 0], bank[6][:]).then_inc(s.xnT_copied, 1)
                        act.wait_ge(s.e_mm, n + 1)
                        nc.scalar.activation(e1[:], bank[1][0:D, 0:POS], ACT.Relu,
                                             bias=par[0:D, b12:b12 + 1]).then_inc(s.e_ready, 1)
                        nc.scalar.activation(e2[:], bank[1][D:2 * D, 0:POS], ACT.Relu,
                                             bias=par[D:2 * D, b12:b12 + 1]).then_inc(s.e_ready, 1)
                        act.wait_ge(s.nmx_ready, n + 1)
                        for ic in range(PC):
                            nc.scalar.activation(prob[:, ic], bank[0][:, ic * POS:(ic + 1) * POS], ACT.Exp,
                                                 bias=nmx[:, ic:ic + 1], accum_out=rsum[:, ic:ic + 1])\
                                .then_inc(s.exp_done, 1)
                        for m in range(K):
                            if m == 0:
                                act.wait_ge(s.a_mm, n * 2 + 1)
                            if m == 2:
                                act.wait_ge(s.pt_mm, n * PC + 1)
                                nc.scalar.copy(probT[:, 0], bank[1][:, 0:POS]).then_inc(s.pt_copied, 1)
                                act.wait_ge(s.a_mm, n * 2 + 2)
                            nc.scalar.activation(rel[:, m], bank[2 + m // 2][:, m % 2 * POS:(m % 2 + 1) * POS],
                                                 ACT.Relu, bias=par[:, b3 + m:b3 + m + 1]).then_inc(s.r_ready, 1)

            def scan_inputs(l, xr):
                act.wait_ge(scan[l].bias, 1)
                for n in (2, 3):
                    for k in range(K):
                        c = k * N + n
                        nc.scalar.activation(inb[:, 1:, k, n * T:(n + 1) * T], xr[:, 1:, k, n * T:(n + 1) * T],
                                             ACT.Identity, bias=bnmr[:, c:c + 1], scale=rstd[:, c:c + 1])\
                            .then_inc(scan[l].inb[n], 1)

            act.wait_ge(s_small, 48)
            attention(0, B12_0, B3_0)
            scan_inputs(1, xw)
            attention(2, B12_2, B3_2)
            scan_inputs(3, xh)

        @block.vector
        def _(dve):
            chain = [0]

            def link(ins):
                chain[0] += 1
                ins.then_inc(s_dve, 1)
                dve.wait_ge(s_dve, chain[0])

            def group_norm(l):
                s = norm[l]
                dve.wait_ge(s.mean, 1)
                link(nc.vector.tensor_copy(gmean[:], bank[4][:, 0:NC]))
                link(nc.vector.tensor_tensor(dev[:], st[:, :, :, 1],
                                             gmean[:].unsqueeze(2).to_broadcast([P, NC, 2]), ALU.subtract))
                link(nc.vector.tensor_tensor(dev2[:], dev[:], dev[:], ALU.mult))
                nc.vector.scalar_tensor_tensor(vadd[:], st[:, :, :, 2], 2.0 / POS, dev2[:],
                                               ALU.mult, ALU.add).then_inc(s.vadd, 1)
                dve.wait_ge(s.var, 1)
                nc.vector.tensor_scalar(gvar[:], bank[5][:, 0:NC], EPS, None, ALU.add).then_inc(s.gvar, 1)
                dve.wait_ge(s.rstd, 1)
                nc.vector.scalar_tensor_tensor(nmr[:], gmean[:], -1.0, rstd[:], ALU.mult, ALU.mult)\
                    .then_inc(s.done, 1)

            def attention(l, alpha):
                s = att[l]
                with dve.Fori(0, N // 2) as pair:
                    for h in range(2):
                        n = pair * 2 + h
                        dve.wait_ge(s.xnT_mm, n * PC + 2)
                        nc.vector.tensor_copy(xnT[:, 1], bank[7][:]).then_inc(s.xnT_copied, 1)
                        dve.wait_ge(s.s_mm, n + 1)
                        nc.vector.reduce_max(mx[:], bank[0][:].rearrange("p (c j) -> p c j", c=PC), AX_X)\
                            .then_inc(s.chain, 1)
                        dve.wait_ge(s.chain, n * 2 + 1)
                        nc.vector.tensor_scalar(nmx[:], mx[:], -1.0, None, ALU.mult).then_inc(s.nmx_ready, 1)
                        dve.wait_ge(s.exp_done, (n + 1) * PC)
                        nc.vector.reciprocal(rrec[:], rsum[:]).then_inc(s.chain, 1)
                        dve.wait_ge(s.chain, n * 2 + 2)
                        for ic in range(PC):
                            nc.vector.tensor_scalar(prob[:, ic], prob[:, ic], rrec[:, ic:ic + 1],
                                                    par[:, alpha:alpha + 1], ALU.mult, ALU.mult)\
                                .then_inc(s.p_ready, 1)
                        dve.wait_ge(s.pt_mm, n * PC + 2)
                        nc.vector.tensor_copy(probT[:, 1], bank[0][:, 0:POS]).then_inc(s.pt_copied, 1)
                        for b in range(2):
                            dve.wait_ge(s.o_mm, n * 2 + b + 1)
                            dve.wait_ge(s.r_ready, n * K + 2 * b + 2)
                            nc.vector.tensor_tensor(upd[:, 2 * b:2 * b + 2],
                                                    bank[4 + b][:].rearrange("p (m j) -> p m j", m=2),
                                                    rel[:, 2 * b:2 * b + 2], ALU.add).then_inc(s.u_done, 1)
                        dve.wait_ge(s.u_done, (n + 1) * 2)
                        for k in range(K):
                            split = upd[:, k].rearrange("p (t j) -> p t j", t=T)
                            res = image_in(l, n)[:, k]
                            if l == 0:
                                res = res.rearrange("p (t j) -> p t j", t=T)
                            nc.vector.tensor_tensor(image_out(l, n)[:, k], split, res, ALU.add)\
                                .then_inc(s.x_done, 1)
                        for k in range(K):
                            dve.wait_ge(s.x_done, n * K + k + 1)
                            nc.vector.bn_stats(st[:, k * N + n].rearrange("p a b -> p (a b)"),
                                               image_out(l, n)[:, k]).then_inc(norm[l + 1].stats, 1)

            def scan_layer(l, xr, cb):
                s = scan[l]
                size = UNIT[l]
                dve.wait_ge(norm[l].done, 1)

                def wide(v):
                    return v[:].unsqueeze(2).to_broadcast([P, NC, T])

                x_0 = xr[:, 0].rearrange("p k (n j) -> p (k n) j", j=T)
                s_0 = state[:, 0].rearrange("p k (n j) -> p (k n) j", j=T)
                link(nc.vector.tensor_tensor(s_0, x_0, wide(rstd), ALU.mult))
                nc.vector.tensor_tensor(s_0, s_0, wide(nmr), ALU.add).then_inc(s.first, 1)
                nc.vector.tensor_tensor(bnmr[:].rearrange("p (k n) -> p k n", n=N),
                                        nmr[:].rearrange("p (k n) -> p k n", n=N),
                                        par[:, cb:cb + K].unsqueeze(2).to_broadcast([P, K, N]),
                                        ALU.add).then_inc(s.bias, 1)
                dve.wait_ge(s.bias, 1)
                for n in (0, 1):
                    for k in range(K):
                        c = k * N + n
                        nc.vector.tensor_scalar(inb[:, 1:, k, n * T:(n + 1) * T], xr[:, 1:, k, n * T:(n + 1) * T],
                                                rstd[:, c:c + 1], bnmr[:, c:c + 1], ALU.mult, ALU.add)\
                            .then_inc(s.inb[n], 1)
                link(nc.vector.tensor_scalar(negb[:], par[:, cb:cb + K], -1.0, None, ALU.mult))

                def relu_step(q, t, parity):
                    for m in range(K):
                        dve.wait_ge(s.y[m], q + 1)
                        nc.vector.scalar_tensor_tensor(state[:, t, m], bank[K * parity + m][:, 0:COLS],
                                                       negb[:, m:m + 1], inb[:, t, m], ALU.max, ALU.add)\
                            .then_inc(s.state[m], 1)

                def prelu_step(q, t, parity):
                    for u in range(K // size):
                        ks = slice(u * size, (u + 1) * size)
                        y = bank[(K // size) * parity + u][:, 0:size * COLS].rearrange("p (m c) -> p m c", m=size)
                        dve.wait_ge(s.y[u], q + 1)
                        nc.vector.tensor_tensor(low[:, ks], y, negb[:, ks].unsqueeze(2).to_broadcast([P, size, COLS]),
                                                ALU.max).then_inc(s.parts, 1)
                        nc.vector.scalar_tensor_tensor(lin[:, ks], y, par[:, PA_1:PA_1 + 1], inb[:, t, ks],
                                                       ALU.mult, ALU.add).then_inc(s.parts, 1)
                        dve.wait_ge(s.parts, q * 4 + 2 * u + 2)
                        nc.vector.scalar_tensor_tensor(state[:, t, ks], low[:, ks], oma[:, 0:1], lin[:, ks],
                                                       ALU.mult, ALU.add).then_inc(s.state[u], 1)

                step = prelu_step if l == 1 else relu_step
                for n in range(N):
                    dve.wait_ge(s.inb[n], K)
                step(0, 1, 0)
                with dve.Fori(0, (T - 2) // 2) as i:
                    for h in range(2):
                        step(i * 2 + 1 + h, i * 2 + 2 + h, (1 + h) % 2)
                dve.wait_ge(s.sb, T - 1)
                step(T - 1, T - 2, 1)
                with dve.Fori(0, (T - 2) // 2) as i:
                    last = i * -2 + (T - 3)
                    for h in range(2):
                        step(i * 2 + T + h, last + -h, h % 2)

            for n in range(N):
                dve.wait_ge(s_x[n], 16)
                for k in range(K):
                    nc.vector.bn_stats(st[:, k * N + n].rearrange("p a b -> p (a b)"), x0[:, n, k])\
                        .then_inc(norm[0].stats, 1)
            nc.vector.memset(mhalf[:], -0.5).then_inc(s_mhalf, 1)
            dve.wait_ge(norm[0].stats, NC)
            group_norm(0)
            dve.wait_ge(s_small, 48)
            nc.vector.tensor_scalar(oma[:], par[:, PA_1:PA_1 + 1], -1.0, 1.0, ALU.mult, ALU.add)\
                .then_inc(s_mhalf, 1)
            attention(0, AL_0)
            group_norm(1)
            scan_layer(1, xw, CB_1)
            dve.wait_ge(scan[1].x, T)
            for k in range(K):
                for n in range(N):
                    nc.vector.bn_stats(st[:, k * N + n].rearrange("p a b -> p (a b)"),
                                       xw[:, :, k, n * T:(n + 1) * T]).then_inc(norm[2].stats, 1)
            dve.wait_ge(norm[2].stats, NC)
            group_norm(2)
            attention(2, AL_2)
            group_norm(3)
            scan_layer(3, xh, CB_3)

        @block.gpsimd
        def _(pool):
            def inverse_std(l):
                pool.wait_ge(norm[l].gvar, 1)
                nc.gpsimd.tensor_tensor(rstd[:], gvar[:], mhalf[:], ALU.pow).then_inc(norm[l].rstd, 1)

            def normalise_images(l):
                s = att[l]
                pool.wait_ge(norm[l].done, 1)

                def normalise(n, buf):
                    for k in range(K):
                        dst = xn[buf][:, k]
                        if l == 2:
                            dst = dst.rearrange("p (t j) -> p t j", t=T)
                        nc.gpsimd.tensor_scalar(dst, image_in(l, n)[:, k], rstd[:, k * N + n:k * N + n + 1],
                                                nmr[:, k * N + n:k * N + n + 1], ALU.mult, ALU.add)\
                            .then_inc(s.xn_ready, 1)

                for n in range(N):
                    if n >= 2:
                        pool.wait_ge(s.a_mm, 2 * (n - 1))
                    normalise(n, n % 2)

            def scan_layer(l, xr, cb):
                s = scan[l]
                units = range(K // UNIT[l])
                bias = par[:, cb:cb + K].unsqueeze(2).to_broadcast([P, K, COLS])

                pool.wait_ge(s.first, 1)
                nc.gpsimd.tensor_tensor(inb[:, 0], state[:, 0], bias, ALU.add).then_inc(s.sb, 1)
                with pool.Fori(1, T - 1) as t:
                    for u in units:
                        pool.wait_ge(s.state[u], t)
                    nc.gpsimd.tensor_tensor(inb[:, t], state[:, t], bias, ALU.add).then_inc(s.sb, 1)
                for u in units:
                    pool.wait_ge(s.state[u], T - 1)
                nc.gpsimd.tensor_tensor(xr[:, T - 1], xr[:, T - 1], state[:, T - 1], ALU.add).then_inc(s.x, 1)
                with pool.Fori(0, T - 1) as i:
                    t = i * -1 + (T - 2)
                    for u in units:
                        pool.wait_ge(s.state[u], i + T)
                    nc.gpsimd.tensor_tensor(xr[:, t], xr[:, t], state[:, t], ALU.add).then_inc(s.x, 1)

            pool.wait_ge(s_mhalf, 1)
            inverse_std(0)
            normalise_images(0)
            inverse_std(1)
            scan_layer(1, xw, CB_1)
            inverse_std(2)
            normalise_images(2)
            inverse_std(3)
            scan_layer(3, xh, CB_3)


def kernel(**inputs):
    import numpy as np
    import concourse.bacc as bacc
    from concourse.bass_utils import run_bass_kernel_spmd

    def col(v):
        return np.asarray(v).reshape(K, P).T

    def weight(w):
        w = np.asarray(w)
        return np.ascontiguousarray(w.T.reshape(K, P, w.shape[0]).transpose(1, 0, 2))

    def whole(v):
        return np.repeat(np.asarray(v).reshape(1, 1), P, axis=0)

    i = {k: np.asarray(v) for k, v in inputs.items()}
    par = np.concatenate(
        [np.concatenate([i["L0_conv_b1"], i["L0_conv_b2"]])[:, None], col(i["L0_conv_b3"]), whole(i["L0_conv_alpha"]),
         col(i["L1_conv_conv_b"]), whole(i["L1_conv_prelu_a"]),
         np.concatenate([i["L2_conv_b1"], i["L2_conv_b2"]])[:, None], col(i["L2_conv_b3"]), whole(i["L2_conv_alpha"]),
         col(i["L3_conv_b"])], axis=1)
    group = np.arange(P) // CG
    arrays = {
        "x": np.ascontiguousarray(i["x"].reshape(N, K, P, T, T).transpose(2, 0, 1, 4, 3)).reshape(P, N, K, POS),
        "par": np.ascontiguousarray(par),
        "gavg": ((group[:, None] == group[None, :]) / (2 * CG)).astype(np.float32),
        "ident": np.eye(P, dtype=np.float32),
        "w12_0": weight(np.concatenate([i["L0_conv_w1"], i["L0_conv_w2"]])),
        "w12_2": weight(np.concatenate([i["L2_conv_w1"], i["L2_conv_w2"]])),
        "w3_0": weight(i["L0_conv_w3"]),
        "w3_2": weight(i["L2_conv_w3"]),
        "wc1": weight(i["L1_conv_conv_w"][:, :, 0, i["L1_conv_conv_w"].shape[3] // 2]),
        "wc3": weight(i["L3_conv_W"][:, :, (i["L3_conv_W"].shape[2] - 1) // 2, 0]),
    }
    nc = bacc.Bacc("TRN2", target_bir_lowering=False, num_devices=1)
    aps = {k: nc.dram_tensor(f"in_{k}", v.shape, mybir.dt.from_np(v.dtype), kind="ExternalInput").ap()
           for k, v in arrays.items()}
    aps["out"] = nc.dram_tensor("result", (P, T, K, COLS), F32, kind="ExternalOutput").ap()
    preact_stack(nc, aps)
    r = run_bass_kernel_spmd(nc, [{f"in_{k}": v for k, v in arrays.items()}], core_ids=[0])
    out = r.results[0]["result"].reshape(P, T, K, N, T)
    return np.ascontiguousarray(out.transpose(3, 2, 0, 1, 4)).reshape(N, C, T, T)
```

```python
from contextlib import ExitStack

import concourse.bass as bass
from concourse import mybir
from concourse.alu_op_type import AluOpType as ALU

F32 = mybir.dt.float32
BF16 = mybir.dt.bfloat16
ACT = mybir.ActivationFunctionType
AX_X = mybir.AxisListType.X

P = 128
N = 4
C = 512
K = C // P
T = 16
POS = T * T
PC = POS // P
D = C // 8
G = 32
CG = C // G
COLS = N * T
NC = K * N
EPS = 1e-5

B12_0, B3_0, AL_0, CB_1, PA_1, B12_2, B3_2, AL_2, CB_3, NPAR = 0, 1, 5, 6, 10, 11, 12, 16, 17, 21

PARTS = 3
PAIR = 2
PHASES = [(0, (0,), 0), (0, (0,), 1), (0, (1,), 0), (0, (2,), 0), (0, (1,), 1),
          (1, (0,), 0), (1, (1,), 0), (1, (2,), 0), (0, (2,), 1), (1, (0, 1, 2), 1)]


class NormSems:

    def __init__(self, sem, l):
        self.stats = sem(f"stats_ready{l}")
        self.mean = sem(f"mean_summed{l}")
        self.vadd = sem(f"vadd_ready{l}")
        self.var = sem(f"var_summed{l}")
        self.gvar = sem(f"gvar_ready{l}")
        self.rstd = sem(f"rstd_ready{l}")
        self.done = sem(f"norm_ready{l}")


class AttentionSems:

    def __init__(self, sem, l):
        self.xn_ready = sem(f"xn_ready{l}")
        self.xnT_mm = sem(f"xnT_mm{l}")
        self.xnT_copied = sem(f"xnT_copied{l}")
        self.e_mm = sem(f"e_mm{l}")
        self.e_ready = sem(f"e_ready{l}")
        self.a_mm = sem(f"a_mm{l}")
        self.r_ready = sem(f"r_ready{l}")
        self.s_mm = sem(f"s_mm{l}")
        self.nmx_ready = sem(f"nmx_ready{l}")
        self.exp_done = sem(f"exp_done{l}")
        self.p_ready = sem(f"p_ready{l}")
        self.pt_mm = sem(f"pt_mm{l}")
        self.pt_copied = sem(f"pt_copied{l}")
        self.o_mm = sem(f"o_mm{l}")
        self.u_done = sem(f"u_done{l}")
        self.x_done = sem(f"x_done{l}")
        self.chain = sem(f"softmax_chain{l}")


class ScanSems:

    def __init__(self, sem, l):
        pairs = range(K // PAIR)
        self.w = sem(f"weight_parts_ready{l}")
        self.first = sem(f"first_state{l}")
        self.bias = sem(f"input_bias{l}")
        self.inb = [sem(f"inputs_ready{l}_{n}") for n in range(N)]
        self.y = [sem(f"products_done{l}_{u}") for u in pairs]
        self.terms = [sem(f"low_lin_ready{l}_{u}") for u in pairs]
        self.rest = [sem(f"state_rest_ready{l}_{u}") for u in pairs]
        self.state = [sem(f"state_ready{l}_{u}") for u in pairs]
        self.parts = [sem(f"state_parts_ready{l}_{u}") for u in pairs]
        self.taken = sem(f"state_taken{l}")


def preact_stack(nc, a):
    with ExitStack() as ctx:
        def sb(name, shape, dt=F32):
            return ctx.enter_context(nc.sbuf_tensor(name, shape, dt))

        def sem(name):
            return ctx.enter_context(nc.semaphore(name))

        bank = [ctx.enter_context(nc.psum_tensor(f"bank{b}", [P, 512], F32)) for b in range(8)]

        x0 = sb("x0", [P, N, K, POS])
        par = sb("par", [P, NPAR])
        ident = sb("ident", [P, P])
        gavg = sb("gavg", [P, P])
        w12 = {l: sb(f"w12_{l}", [P, K, 2 * D]) for l in (0, 2)}
        w3 = {l: sb(f"w3_{l}", [P, K, C]) for l in (0, 2)}
        wc = {l: sb(f"wc_{l}", [P, K, C]) for l in (1, 3)}
        w_parts = {l: sb(f"w_parts_{l}", [P, PARTS, K, C], BF16) for l in (1, 3)}

        xw = sb("xw", [P, T, K, COLS])
        xh = sb("xh", [P, T, K, COLS])

        st = sb("st", [P, NC, 2, 3])
        dev = sb("dev", [P, NC, 2])
        dev2 = sb("dev2", [P, NC, 2])
        vadd = sb("vadd", [P, NC, 2])
        gmean = sb("gmean", [P, NC])
        gvar = sb("gvar", [P, NC])
        mhalf = sb("mhalf", [P, NC])
        rstd = sb("rstd", [P, NC])
        nmr = sb("nmr", [P, NC])

        xn = [sb(f"xn{s}", [P, K, POS]) for s in range(2)]
        xnT = sb("xnT", [P, PC, C])
        e1 = sb("e1", [D, POS])
        e2 = sb("e2", [D, POS])
        prob = sb("prob", [P, PC, POS])
        probT = sb("probT", [P, PC, POS])
        mx = sb("mx", [P, PC])
        nmx = sb("nmx", [P, PC])
        rsum = sb("rsum", [P, PC])
        rrec = sb("rrec", [P, PC])
        rel = sb("rel", [P, K, POS])
        upd = sb("upd", [P, K, POS])

        state = sb("state", [P, 2, K, COLS])
        inb = sb("inb", [P, T, K, COLS])
        low = sb("low", [P, K, COLS])
        lin = sb("lin", [P, K, COLS])
        rest = sb("rest", [P, K, COLS])
        s_parts = sb("s_parts", [P, 2, PARTS, K, COLS], BF16)
        negb = sb("negb", [P, K])
        bnmr = sb("bnmr", [P, NC])
        oma = sb("oma", [P, 1])

        s_x = [sem(f"x_loaded{n}") for n in range(N)]
        s_small = sem("small_loaded")
        s_w12 = {l: sem(f"w12_loaded{l}") for l in (0, 2)}
        s_w3 = {l: sem(f"w3_loaded{l}") for l in (0, 2)}
        s_wc = {l: sem(f"wc_loaded{l}") for l in (1, 3)}
        s_rest = {l: sem(f"weight_rest_ready{l}") for l in (1, 3)}
        s_mhalf = sem("mhalf_set")
        s_out = sem("out_stored")

        norm = [NormSems(sem, l) for l in range(4)]
        att = {l: AttentionSems(sem, l) for l in (0, 2)}
        scan = {l: ScanSems(sem, l) for l in (1, 3)}
        s_dve = sem("vector_chain")

        def image_in(l, n):
            if l == 0:
                return x0[:, n]
            return xw.rearrange("p w k (n h) -> p n k h w", n=N)[:, n]

        def image_out(l, n):
            dst = xw if l == 0 else xh
            return dst.rearrange("p t k (n j) -> p n k t j", n=N)[:, n]

        block = ctx.enter_context(nc.Block())

        @block.sync
        def _(sp):
            sp.dma_start(par[:], a["par"]).then_inc(s_small, 16)
            sp.dma_start(gavg[:], a["gavg"]).then_inc(s_small, 16)
            sp.dma_start(ident[:], a["ident"]).then_inc(s_small, 16)
            for n in range(N):
                sp.dma_start(x0[:, n], a["x"][:, n]).then_inc(s_x[n], 16)
            sp.dma_start(wc[1][:], a["wc1"]).then_inc(s_wc[1], 16)
            sp.dma_start(wc[3][:], a["wc3"]).then_inc(s_wc[3], 16)
            with sp.Fori(0, T) as i:
                t = i * -1 + (T - 1)
                sp.wait_ge(scan[3].taken, i + T)
                sp.dma_start(a["out"][:, t], xh[:, t]).then_inc(s_out, 16)
            sp.wait_ge(s_out, 16 * T)

        @block.tensor
        def _(pe):
            def group_norm(l):
                s = norm[l]
                pe.wait_ge(s.stats, NC)
                if l == 0:
                    pe.wait_ge(s_small, 48)
                nc.tensor.matmul(bank[4][:, 0:NC], gavg[:], st[:, :, 0, 1], start=True, stop=False)
                nc.tensor.matmul(bank[4][:, 0:NC], gavg[:], st[:, :, 1, 1], start=False, stop=True)\
                    .then_inc(s.mean, 1)
                pe.wait_ge(s.vadd, 1)
                nc.tensor.matmul(bank[5][:, 0:NC], gavg[:], vadd[:, :, 0], start=True, stop=False)
                nc.tensor.matmul(bank[5][:, 0:NC], gavg[:], vadd[:, :, 1], start=False, stop=True)\
                    .then_inc(s.var, 1)

            def attention(l):
                s = att[l]
                pe.wait_ge(s_w12[l], 16)
                pe.wait_ge(s_w3[l], 16)

                def relu_branch(xn_s, m, done):
                    for k in range(K):
                        mm = nc.tensor.matmul(bank[2 + m // 2][:, m % 2 * POS:(m % 2 + 1) * POS],
                                              w3[l][:, k, m * P:(m + 1) * P], xn_s[:, k],
                                              start=(k == 0), stop=(k == K - 1))
                    if done:
                        mm.then_inc(s.a_mm, 1)

                with pe.Fori(0, N // 2) as pair:
                    for h in range(2):
                        n = pair * 2 + h
                        pe.wait_ge(s.xn_ready, (n + 1) * K)
                        for pc in range(PC):
                            for k in range(K):
                                mm = nc.tensor.transpose(bank[6 + pc][:, k * P:(k + 1) * P],
                                                         xn[h][:, k, pc * P:(pc + 1) * P], ident[:])
                            mm.then_inc(s.xnT_mm, 1)
                        for k in range(K):
                            mm = nc.tensor.matmul(bank[1][:, 0:POS], w12[l][:, k], xn[h][:, k],
                                                  start=(k == 0), stop=(k == K - 1))
                        mm.then_inc(s.e_mm, 1)
                        relu_branch(xn[h], 0, False)
                        pe.wait_ge(s.e_ready, (n + 1) * 2)
                        for ic in range(PC):
                            mm = nc.tensor.matmul(bank[0][:, ic * POS:(ic + 1) * POS],
                                                  e1[:, ic * P:(ic + 1) * P], e2[:], start=True, stop=True)
                        mm.then_inc(s.s_mm, 1)
                        relu_branch(xn[h], 1, True)
                        relu_branch(xn[h], 2, False)
                        pe.wait_ge(s.p_ready, (n + 1) * PC)
                        for jc in range(PC):
                            for ic in range(PC):
                                mm = nc.tensor.transpose(bank[1 - jc][:, ic * P:(ic + 1) * P],
                                                         prob[:, ic, jc * P:(jc + 1) * P], ident[:])
                            mm.then_inc(s.pt_mm, 1)
                        relu_branch(xn[h], 3, True)
                        pe.wait_ge(s.xnT_copied, (n + 1) * PC)
                        pe.wait_ge(s.pt_copied, (n + 1) * PC)
                        for m in range(K):
                            for jc in range(PC):
                                mm = nc.tensor.matmul(bank[4 + m // 2][:, m % 2 * POS:(m % 2 + 1) * POS],
                                                      xnT[:, jc, m * P:(m + 1) * P], probT[:, jc],
                                                      start=(jc == 0), stop=(jc == PC - 1))
                            if m % 2:
                                mm.then_inc(s.o_mm, 1)
                            if m == 1:
                                pe.wait_ge(s.r_ready, (n + 1) * K)

            def scan_layer(l):
                s = scan[l]
                pe.wait_ge(s.w, PARTS)

                def step(q, h):
                    seen = set()
                    for j, (u, parts, v) in enumerate(PHASES):
                        first = all(o[2] != v for o in PHASES[:j])
                        final = all(o[2] != v for o in PHASES[j + 1:])
                        todo = [(k, m, wp, part) for m in range(PAIR) for k in range(u * PAIR, (u + 1) * PAIR)
                                for wp in range(PARTS) for part in parts]
                        for n, (k, m, wp, part) in enumerate(todo):
                            if (u, part) not in seen:
                                pe.wait_ge(s.parts[u], q * PARTS + part + 1)
                                seen.add((u, part))
                            c = v * PAIR + m
                            mm = nc.tensor.matmul(
                                bank[(K // PAIR) * h + v][:, m * COLS:(m + 1) * COLS],
                                w_parts[l][:, wp, k, c * P:(c + 1) * P], s_parts[:, h, part, k],
                                start=first and n == 0, stop=final and n == len(todo) - 1, skip_group_check=True)
                        if final:
                            mm.then_inc(s.y[v], 1)

                with pe.Fori(0, T - 1) as i:
                    for h in range(2):
                        step(i * 2 + h, h)

            group_norm(0)
            attention(0)
            group_norm(1)
            scan_layer(1)
            group_norm(2)
            attention(2)
            group_norm(3)
            scan_layer(3)

        @block.scalar
        def _(act):
            for l in (0, 2):
                act.dma_start(w12[l][:], a[f"w12_{l}"]).then_inc(s_w12[l], 16)
                act.dma_start(w3[l][:], a[f"w3_{l}"]).then_inc(s_w3[l], 16)

            def attention(l, b12, b3):
                s = att[l]
                with act.Fori(0, N // 2) as pair:
                    for h in range(2):
                        n = pair * 2 + h
                        act.wait_ge(s.xnT_mm, n * PC + 1)
                        nc.scalar.copy(xnT[:, 0], bank[6][:]).then_inc(s.xnT_copied, 1)
                        act.wait_ge(s.e_mm, n + 1)
                        nc.scalar.activation(e1[:], bank[1][0:D, 0:POS], ACT.Relu,
                                             bias=par[0:D, b12:b12 + 1]).then_inc(s.e_ready, 1)
                        nc.scalar.activation(e2[:], bank[1][D:2 * D, 0:POS], ACT.Relu,
                                             bias=par[D:2 * D, b12:b12 + 1]).then_inc(s.e_ready, 1)
                        act.wait_ge(s.nmx_ready, n + 1)
                        for ic in range(PC):
                            nc.scalar.activation(prob[:, ic], bank[0][:, ic * POS:(ic + 1) * POS], ACT.Exp,
                                                 bias=nmx[:, ic:ic + 1], accum_out=rsum[:, ic:ic + 1])\
                                .then_inc(s.exp_done, 1)
                        for m in range(K):
                            if m == 0:
                                act.wait_ge(s.a_mm, n * 2 + 1)
                            if m == 2:
                                act.wait_ge(s.pt_mm, n * PC + 1)
                                nc.scalar.copy(probT[:, 0], bank[1][:, 0:POS]).then_inc(s.pt_copied, 1)
                                act.wait_ge(s.a_mm, n * 2 + 2)
                            nc.scalar.activation(rel[:, m], bank[2 + m // 2][:, m % 2 * POS:(m % 2 + 1) * POS],
                                                 ACT.Relu, bias=par[:, b3 + m:b3 + m + 1]).then_inc(s.r_ready, 1)

            def scan_inputs(l, xr):
                act.wait_ge(scan[l].bias, 1)
                for n in (2, 3):
                    for k in range(K):
                        c = k * N + n
                        nc.scalar.activation(inb[:, 1:, k, n * T:(n + 1) * T], xr[:, 1:, k, n * T:(n + 1) * T],
                                             ACT.Identity, bias=bnmr[:, c:c + 1], scale=rstd[:, c:c + 1])\
                            .then_inc(scan[l].inb[n], 1)

            act.wait_ge(s_small, 48)
            attention(0, B12_0, B3_0)
            scan_inputs(1, xw)
            attention(2, B12_2, B3_2)
            scan_inputs(3, xh)

        @block.vector
        def _(dve):
            chain = [0]

            def link(ins):
                chain[0] += 1
                ins.then_inc(s_dve, 1)
                dve.wait_ge(s_dve, chain[0])

            def group_norm(l):
                s = norm[l]
                dve.wait_ge(s.mean, 1)
                link(nc.vector.tensor_copy(gmean[:], bank[4][:, 0:NC]))
                link(nc.vector.tensor_tensor(dev[:], st[:, :, :, 1],
                                             gmean[:].unsqueeze(2).to_broadcast([P, NC, 2]), ALU.subtract))
                link(nc.vector.tensor_tensor(dev2[:], dev[:], dev[:], ALU.mult))
                nc.vector.scalar_tensor_tensor(vadd[:], st[:, :, :, 2], 2.0 / POS, dev2[:],
                                               ALU.mult, ALU.add).then_inc(s.vadd, 1)
                dve.wait_ge(s.var, 1)
                nc.vector.tensor_scalar(gvar[:], bank[5][:, 0:NC], EPS, None, ALU.add).then_inc(s.gvar, 1)
                dve.wait_ge(s.rstd, 1)
                nc.vector.scalar_tensor_tensor(nmr[:], gmean[:], -1.0, rstd[:], ALU.mult, ALU.mult)\
                    .then_inc(s.done, 1)

            def attention(l, alpha):
                s = att[l]
                with dve.Fori(0, N // 2) as pair:
                    for h in range(2):
                        n = pair * 2 + h
                        dve.wait_ge(s.xnT_mm, n * PC + 2)
                        nc.vector.tensor_copy(xnT[:, 1], bank[7][:]).then_inc(s.xnT_copied, 1)
                        dve.wait_ge(s.s_mm, n + 1)
                        nc.vector.reduce_max(mx[:], bank[0][:].rearrange("p (c j) -> p c j", c=PC), AX_X)\
                            .then_inc(s.chain, 1)
                        dve.wait_ge(s.chain, n * 2 + 1)
                        nc.vector.tensor_scalar(nmx[:], mx[:], -1.0, None, ALU.mult).then_inc(s.nmx_ready, 1)
                        dve.wait_ge(s.exp_done, (n + 1) * PC)
                        nc.vector.reciprocal(rrec[:], rsum[:]).then_inc(s.chain, 1)
                        dve.wait_ge(s.chain, n * 2 + 2)
                        for ic in range(PC):
                            nc.vector.tensor_scalar(prob[:, ic], prob[:, ic], rrec[:, ic:ic + 1],
                                                    par[:, alpha:alpha + 1], ALU.mult, ALU.mult)\
                                .then_inc(s.p_ready, 1)
                        dve.wait_ge(s.pt_mm, n * PC + 2)
                        nc.vector.tensor_copy(probT[:, 1], bank[0][:, 0:POS]).then_inc(s.pt_copied, 1)
                        for b in range(2):
                            dve.wait_ge(s.o_mm, n * 2 + b + 1)
                            dve.wait_ge(s.r_ready, n * K + 2 * b + 2)
                            nc.vector.tensor_tensor(upd[:, 2 * b:2 * b + 2],
                                                    bank[4 + b][:].rearrange("p (m j) -> p m j", m=2),
                                                    rel[:, 2 * b:2 * b + 2], ALU.add).then_inc(s.u_done, 1)
                        dve.wait_ge(s.u_done, (n + 1) * 2)
                        for k in range(K):
                            split = upd[:, k].rearrange("p (t j) -> p t j", t=T)
                            res = image_in(l, n)[:, k]
                            if l == 0:
                                res = res.rearrange("p (t j) -> p t j", t=T)
                            nc.vector.tensor_tensor(image_out(l, n)[:, k], split, res, ALU.add)\
                                .then_inc(s.x_done, 1)
                        for k in range(K):
                            dve.wait_ge(s.x_done, n * K + k + 1)
                            nc.vector.bn_stats(st[:, k * N + n].rearrange("p a b -> p (a b)"),
                                               image_out(l, n)[:, k]).then_inc(norm[l + 1].stats, 1)

            def scan_layer(l, xr, cb):
                s = scan[l]
                dve.wait_ge(norm[l].done, 1)

                def wide(v):
                    return v[:].unsqueeze(2).to_broadcast([P, NC, T])

                x_0 = xr[:, 0].rearrange("p k (n j) -> p (k n) j", j=T)
                s_0 = state[:, 0].rearrange("p k (n j) -> p (k n) j", j=T)
                link(nc.vector.tensor_tensor(s_0, x_0, wide(rstd), ALU.mult))
                nc.vector.tensor_tensor(s_0, s_0, wide(nmr), ALU.add).then_inc(s.first, 1)
                dve.wait_ge(s.first, 1)
                split = s_parts[:, 0]
                link(nc.vector.tensor_copy(split[:, 0], state[:, 0]))
                for u in range(K // PAIR):
                    dve.sem_inc(s.parts[u], 1)
                link(nc.vector.tensor_tensor(rest[:], state[:, 0], split[:, 0], ALU.subtract))
                link(nc.vector.tensor_copy(split[:, 1], rest[:]))
                for u in range(K // PAIR):
                    dve.sem_inc(s.parts[u], 1)
                link(nc.vector.tensor_tensor(split[:, 2], rest[:], split[:, 1], ALU.subtract))
                for u in range(K // PAIR):
                    dve.sem_inc(s.parts[u], 1)
                nc.vector.tensor_tensor(bnmr[:].rearrange("p (k n) -> p k n", n=N),
                                        nmr[:].rearrange("p (k n) -> p k n", n=N),
                                        par[:, cb:cb + K].unsqueeze(2).to_broadcast([P, K, N]),
                                        ALU.add).then_inc(s.bias, 1)
                dve.wait_ge(s.bias, 1)
                for n in (0, 1):
                    for k in range(K):
                        c = k * N + n
                        nc.vector.tensor_scalar(inb[:, 1:, k, n * T:(n + 1) * T], xr[:, 1:, k, n * T:(n + 1) * T],
                                                rstd[:, c:c + 1], bnmr[:, c:c + 1], ALU.mult, ALU.add)\
                            .then_inc(s.inb[n], 1)
                link(nc.vector.tensor_scalar(negb[:], par[:, cb:cb + K], -1.0, None, ALU.mult))

                def chunks(u):
                    return slice(u * PAIR, (u + 1) * PAIR)

                def product(u, h):
                    return bank[(K // PAIR) * h + u][:, 0:PAIR * COLS].rearrange("p (m c) -> p m c", m=PAIR)

                def relu_state(q, t, h, u):
                    dve.wait_ge(s.y[u], q + 1)
                    for k in range(u * PAIR, (u + 1) * PAIR):
                        last = nc.vector.scalar_tensor_tensor(
                            state[:, 1 - h, k], product(u, h)[:, k % PAIR], negb[:, k:k + 1], inb[:, t, k],
                            ALU.max, ALU.add)
                    last.then_inc(s.state[u], 1)
                    dve.wait_ge(s.state[u], q + 1)
                    nc.vector.tensor_copy(s_parts[:, 1 - h, 0, chunks(u)], state[:, 1 - h, chunks(u)])\
                        .then_inc(s.parts[u], 1)

                def prelu_low(q, t, h, u):
                    dve.wait_ge(s.y[u], q + 1)
                    nc.vector.tensor_tensor(low[:, chunks(u)], product(u, h),
                                            negb[:, chunks(u)].unsqueeze(2).to_broadcast([P, PAIR, COLS]),
                                            ALU.max).then_inc(s.terms[u], 1)

                def prelu_lin(q, t, h, u):
                    nc.vector.scalar_tensor_tensor(lin[:, chunks(u)], product(u, h), par[:, PA_1:PA_1 + 1],
                                                   inb[:, t, chunks(u)], ALU.mult, ALU.add)\
                        .then_inc(s.terms[u], 1)

                def prelu_first_part(q, t, h, u):
                    dve.wait_ge(s.terms[u], q * 2 + 2)
                    nc.vector.scalar_tensor_tensor(s_parts[:, 1 - h, 0, chunks(u)], low[:, chunks(u)], oma[:, 0:1],
                                                   lin[:, chunks(u)], ALU.mult, ALU.add).then_inc(s.parts[u], 1)

                def prelu_state(q, t, h, u):
                    nc.vector.scalar_tensor_tensor(state[:, 1 - h, chunks(u)], low[:, chunks(u)], oma[:, 0:1],
                                                   lin[:, chunks(u)], ALU.mult, ALU.add).then_inc(s.state[u], 1)

                def split_rest(q, t, h, u):
                    dve.wait_ge(s.parts[u], (q + 1) * PARTS + 1)
                    if l == 1:
                        dve.wait_ge(s.state[u], q + 1)
                    nc.vector.tensor_tensor(rest[:, chunks(u)], state[:, 1 - h, chunks(u)],
                                            s_parts[:, 1 - h, 0, chunks(u)], ALU.subtract).then_inc(s.rest[u], 1)

                def split_second(q, t, h, u):
                    dve.wait_ge(s.rest[u], q + 1)
                    nc.vector.tensor_copy(s_parts[:, 1 - h, 1, chunks(u)], rest[:, chunks(u)])\
                        .then_inc(s.parts[u], 1)

                def split_third(q, t, h, u):
                    dve.wait_ge(s.parts[u], (q + 1) * PARTS + 2)
                    nc.vector.tensor_tensor(s_parts[:, 1 - h, 2, chunks(u)], rest[:, chunks(u)],
                                            s_parts[:, 1 - h, 1, chunks(u)], ALU.subtract).then_inc(s.parts[u], 1)

                split = [(split_rest, 0), (split_second, 0), (split_third, 0),
                         (split_rest, 1), (split_second, 1), (split_third, 1)]
                stages = {
                    1: [(prelu_low, 0), (prelu_lin, 0), (prelu_first_part, 0), (prelu_state, 0),
                        (split_rest, 0), (prelu_low, 1), (split_second, 0), (prelu_lin, 1), (split_third, 0),
                        (prelu_first_part, 1), (prelu_state, 1)] + split[3:],
                    3: [(relu_state, 0)] + split[:3] + [(relu_state, 1)] + split[3:]}[l]

                def step(q, t, h):
                    if not (isinstance(q, int) and q == 0):
                        dve.wait_ge(s.taken, q)
                    for stage, u in stages:
                        stage(q, t, h, u)

                for n in range(N):
                    dve.wait_ge(s.inb[n], K)
                step(0, 1, 0)
                with dve.Fori(0, (T - 2) // 2) as i:
                    for h in range(2):
                        step(i * 2 + 1 + h, i * 2 + 2 + h, 1 - h)
                dve.wait_ge(s.taken, T - 1)
                step(T - 1, T - 2, 1)
                with dve.Fori(0, (T - 2) // 2) as i:
                    last = i * -2 + (T - 3)
                    for h in range(2):
                        step(i * 2 + T + h, last + -h, h)

            for n in range(N):
                dve.wait_ge(s_x[n], 16)
                for k in range(K):
                    nc.vector.bn_stats(st[:, k * N + n].rearrange("p a b -> p (a b)"), x0[:, n, k])\
                        .then_inc(norm[0].stats, 1)
            nc.vector.memset(mhalf[:], -0.5).then_inc(s_mhalf, 1)
            dve.wait_ge(norm[0].stats, NC)
            group_norm(0)
            dve.wait_ge(s_small, 48)
            nc.vector.tensor_scalar(oma[:], par[:, PA_1:PA_1 + 1], -1.0, 1.0, ALU.mult, ALU.add)\
                .then_inc(s_mhalf, 1)
            attention(0, AL_0)
            group_norm(1)
            scan_layer(1, xw, CB_1)
            dve.wait_ge(scan[1].taken, 2 * T - 1)
            for k in range(K):
                for n in range(N):
                    nc.vector.bn_stats(st[:, k * N + n].rearrange("p a b -> p (a b)"),
                                       xw[:, :, k, n * T:(n + 1) * T]).then_inc(norm[2].stats, 1)
            dve.wait_ge(norm[2].stats, NC)
            group_norm(2)
            attention(2, AL_2)
            group_norm(3)
            scan_layer(3, xh, CB_3)

        @block.gpsimd
        def _(pool):
            def inverse_std(l):
                pool.wait_ge(norm[l].gvar, 1)
                nc.gpsimd.tensor_tensor(rstd[:], gvar[:], mhalf[:], ALU.pow).then_inc(norm[l].rstd, 1)

            def normalise_images(l):
                s = att[l]
                pool.wait_ge(norm[l].done, 1)

                def normalise(n, buf):
                    for k in range(K):
                        dst = xn[buf][:, k]
                        if l == 2:
                            dst = dst.rearrange("p (t j) -> p t j", t=T)
                        nc.gpsimd.tensor_scalar(dst, image_in(l, n)[:, k], rstd[:, k * N + n:k * N + n + 1],
                                                nmr[:, k * N + n:k * N + n + 1], ALU.mult, ALU.add)\
                            .then_inc(s.xn_ready, 1)

                for n in range(N):
                    if n >= 2:
                        pool.wait_ge(s.a_mm, 2 * (n - 1))
                    normalise(n, n % 2)

            def split_weights(l):
                s = scan[l]
                pool.wait_ge(s_wc[l], 16)
                w = wc[l]
                nc.gpsimd.tensor_copy(w_parts[l][:, 0], w[:]).then_inc(s.w, 1)
                pool.wait_ge(s.w, 1)
                nc.gpsimd.tensor_tensor(w[:], w[:], w_parts[l][:, 0], ALU.subtract).then_inc(s_rest[l], 1)
                pool.wait_ge(s_rest[l], 1)
                nc.gpsimd.tensor_copy(w_parts[l][:, 1], w[:]).then_inc(s.w, 1)
                pool.wait_ge(s.w, 2)
                nc.gpsimd.tensor_tensor(w_parts[l][:, 2], w[:], w_parts[l][:, 1], ALU.subtract).then_inc(s.w, 1)

            def scan_layer(l, xr, cb):
                s = scan[l]
                pairs = range(K // PAIR)
                bias = par[:, cb:cb + K].unsqueeze(2).to_broadcast([P, K, COLS])

                pool.wait_ge(s.first, 1)
                nc.gpsimd.tensor_tensor(inb[:, 0], state[:, 0], bias, ALU.add).then_inc(s.taken, 1)
                with pool.Fori(0, (T - 2) // 2) as i:
                    for h in range(2):
                        t = i * 2 + 1 + h
                        for u in pairs:
                            pool.wait_ge(s.state[u], t)
                        nc.gpsimd.tensor_tensor(inb[:, t], state[:, 1 - h], bias, ALU.add).then_inc(s.taken, 1)

                def add_state(j, t, h):
                    for u in pairs:
                        pool.wait_ge(s.state[u], j)
                    nc.gpsimd.tensor_tensor(xr[:, t], xr[:, t], state[:, h], ALU.add).then_inc(s.taken, 1)

                add_state(T - 1, T - 1, 1)
                with pool.Fori(0, (T - 2) // 2) as i:
                    last = i * -2 + (T - 2)
                    for h in range(2):
                        add_state(i * 2 + T + h, last + -h, h)
                add_state(2 * T - 2, 0, 0)

            pool.wait_ge(s_mhalf, 1)
            inverse_std(0)
            normalise_images(0)
            split_weights(1)
            inverse_std(1)
            scan_layer(1, xw, CB_1)
            inverse_std(2)
            normalise_images(2)
            split_weights(3)
            inverse_std(3)
            scan_layer(3, xh, CB_3)


def kernel(**inputs):
    import numpy as np
    import concourse.bacc as bacc
    from concourse.bass_utils import run_bass_kernel_spmd

    def col(v):
        return np.asarray(v).reshape(K, P).T

    def weight(w):
        w = np.asarray(w)
        return np.ascontiguousarray(w.T.reshape(K, P, w.shape[0]).transpose(1, 0, 2))

    def whole(v):
        return np.repeat(np.asarray(v).reshape(1, 1), P, axis=0)

    i = {k: np.asarray(v) for k, v in inputs.items()}
    par = np.concatenate(
        [np.concatenate([i["L0_conv_b1"], i["L0_conv_b2"]])[:, None], col(i["L0_conv_b3"]), whole(i["L0_conv_alpha"]),
         col(i["L1_conv_conv_b"]), whole(i["L1_conv_prelu_a"]),
         np.concatenate([i["L2_conv_b1"], i["L2_conv_b2"]])[:, None], col(i["L2_conv_b3"]), whole(i["L2_conv_alpha"]),
         col(i["L3_conv_b"])], axis=1)
    group = np.arange(P) // CG
    arrays = {
        "x": np.ascontiguousarray(i["x"].reshape(N, K, P, T, T).transpose(2, 0, 1, 4, 3)).reshape(P, N, K, POS),
        "par": np.ascontiguousarray(par),
        "gavg": ((group[:, None] == group[None, :]) / (2 * CG)).astype(np.float32),
        "ident": np.eye(P, dtype=np.float32),
        "w12_0": weight(np.concatenate([i["L0_conv_w1"], i["L0_conv_w2"]])),
        "w12_2": weight(np.concatenate([i["L2_conv_w1"], i["L2_conv_w2"]])),
        "w3_0": weight(i["L0_conv_w3"]),
        "w3_2": weight(i["L2_conv_w3"]),
        "wc1": weight(i["L1_conv_conv_w"][:, :, 0, i["L1_conv_conv_w"].shape[3] // 2]),
        "wc3": weight(i["L3_conv_W"][:, :, (i["L3_conv_W"].shape[2] - 1) // 2, 0]),
    }
    nc = bacc.Bacc("TRN2", target_bir_lowering=False, num_devices=1)
    aps = {k: nc.dram_tensor(f"in_{k}", v.shape, mybir.dt.from_np(v.dtype), kind="ExternalInput").ap()
           for k, v in arrays.items()}
    aps["out"] = nc.dram_tensor("result", (P, T, K, COLS), F32, kind="ExternalOutput").ap()
    preact_stack(nc, aps)
    r = run_bass_kernel_spmd(nc, [{f"in_{k}": v for k, v in arrays.items()}], core_ids=[0])
    out = r.results[0]["result"].reshape(P, T, K, N, T)
    return np.ascontiguousarray(out.transpose(3, 2, 0, 1, 4)).reshape(N, C, T, T)
```

```python
from contextlib import ExitStack

import concourse.bass as bass
from concourse import mybir
from concourse.alu_op_type import AluOpType as ALU

F32 = mybir.dt.float32
BF16 = mybir.dt.bfloat16
ACT = mybir.ActivationFunctionType
AX_X = mybir.AxisListType.X

P = 128
N = 4
C = 512
K = C // P
T = 16
POS = T * T
PC = POS // P
D = C // 8
G = 32
CG = C // G
COLS = N * T
NC = N * K
EPS = 1e-5

B12_0, B3_0, AL_0, CB_1, PA_1, B12_2, B3_2, AL_2, CB_3, NPAR = 0, 1, 5, 6, 10, 11, 12, 16, 17, 21

SETS = 2

WARM_STATS = [9, 6, 12, 6]
WARM_MEANS = [3, 3, 3, 3]
WARM_VARIANCES = [11, 11, 9, 11]

PARTS = 3
PAIR = 2
PHASES = {
    1: [(0, (0,), 0), (0, (0,), 1), (0, (1,), 0), (0, (1,), 1), (0, (2,), 0),
        (1, (0,), 0), (1, (1,), 0), (1, (2,), 0), (0, (2,), 1), (1, (0, 1, 2), 1)],
    3: [(0, (0,), 0), (0, (0,), 1), (0, (1,), 0), (0, (2,), 0), (0, (1,), 1),
        (1, (0,), 0), (1, (1,), 0), (1, (2,), 0), (0, (2,), 1), (1, (0, 1, 2), 1)]}


class NormSems:

    def __init__(self, sem, l):
        self.stats = sem(f"stats_ready{l}")
        self.mean = sem(f"mean_summed{l}")
        self.vadd = sem(f"set_variances_ready{l}")
        self.var = sem(f"var_summed{l}")
        self.gvar = sem(f"gvar_ready{l}")
        self.rstd = sem(f"rstd_ready{l}")
        self.neg = sem(f"mean_negated{l}")
        self.std = sem(f"root_ready{l}")
        self.done = sem(f"norm_ready{l}")


class AttentionSems:

    def __init__(self, sem, l):
        self.xn_ready = sem(f"xn_ready{l}")
        self.xnT_mm = sem(f"xnT_mm{l}")
        self.xnT_copied = sem(f"xnT_copied{l}")
        self.e_mm = sem(f"e_mm{l}")
        self.e_ready = sem(f"e_ready{l}")
        self.a_mm = sem(f"a_mm{l}")
        self.r_ready = sem(f"r_ready{l}")
        self.s_mm = sem(f"s_mm{l}")
        self.nmx_ready = sem(f"nmx_ready{l}")
        self.exp_done = sem(f"exp_done{l}")
        self.p_ready = sem(f"p_ready{l}")
        self.pt_mm = sem(f"pt_mm{l}")
        self.pt_copied = sem(f"pt_copied{l}")
        self.o_mm = sem(f"o_mm{l}")
        self.rx_done = sem(f"rx_done{l}")
        self.x_done = sem(f"x_done{l}")
        self.chain = sem(f"softmax_chain{l}")


class ScanSems:

    def __init__(self, sem, l):
        pairs = range(K // PAIR)
        self.w = sem(f"weight_parts_ready{l}")
        self.scaled = sem(f"first_state_scaled{l}")
        self.first = sem(f"first_state{l}")
        self.first_rest = sem(f"first_state_rest{l}")
        self.bias = sem(f"input_bias{l}")
        self.inb = sem(f"inputs_ready{l}")
        self.y = [sem(f"products_done{l}_{u}") for u in pairs]
        self.terms = [sem(f"low_lin_ready{l}_{u}") for u in pairs]
        self.rest = [sem(f"state_rest_ready{l}_{u}") for u in pairs]
        self.state = [sem(f"state_ready{l}_{u}") for u in pairs]
        self.parts = [sem(f"state_parts_ready{l}_{u}") for u in pairs]
        self.taken = sem(f"state_taken{l}")
        self.last_in = sem(f"last_input{l}")
        self.result = sem(f"last_strip_done{l}")


def preact_stack(nc, a):
    with ExitStack() as ctx:
        def sb(name, shape, dt=F32):
            return ctx.enter_context(nc.sbuf_tensor(name, shape, dt))

        def sem(name):
            return ctx.enter_context(nc.semaphore(name))

        bank = [ctx.enter_context(nc.psum_tensor(f"bank{b}", [P, 512], F32)) for b in range(8)]

        x0 = sb("x0", [P, N, K, POS])
        par = sb("par", [P, NPAR])
        ident = sb("ident", [P, P])
        gavg = sb("gavg", [P, P])
        w12 = {l: sb(f"w12_{l}", [P, K, 2 * D]) for l in (0, 2)}
        w3 = {l: sb(f"w3_{l}", [P, K, C]) for l in (0, 2)}
        wc = {l: sb(f"wc_{l}", [P, K, C]) for l in (1, 3)}
        w_parts = {l: sb(f"w_parts_{l}", [P, PARTS, K, C], BF16) for l in (1, 3)}

        xw = sb("xw", [P, T, K, COLS])
        xh = sb("xh", [P, T, K, COLS])

        st = sb("st", [P, NC, SETS, 3])
        svar = sb("svar", [P, NC, SETS])
        dev = sb("dev", [P, NC, SETS])
        dev2 = sb("dev2", [P, NC, SETS])
        vadd = sb("vadd", [P, NC, SETS])
        gmean = sb("gmean", [P, NC])
        gvar = sb("gvar", [P, NC])
        root = sb("root", [P, NC])
        inv = sb("inv", [P, NC])
        half = sb("half", [P, NC])
        err = sb("err", [P, NC])
        mhalf = sb("mhalf", [P, NC])
        rstd = sb("rstd", [P, NC])
        gneg = sb("gneg", [P, NC])
        nmr = sb("nmr", [P, NC])
        zeros = sb("zeros", [P, 512], BF16)
        warm = sb("warm", [P, 1])

        xn = [sb(f"xn{s}", [P, K, POS]) for s in range(2)]
        xnT = sb("xnT", [P, PC, C])
        e1 = sb("e1", [D, POS])
        e2 = sb("e2", [D, POS])
        prob = sb("prob", [P, PC, POS])
        probT = sb("probT", [P, PC, POS])
        mx = sb("mx", [P, PC])
        nmx = sb("nmx", [P, PC])
        rsum = sb("rsum", [P, PC])
        rrec = sb("rrec", [P, PC])
        rel = sb("rel", [P, K, POS])
        rx = sb("rx", [P, K, POS])

        state = sb("state", [P, 2, K, COLS])
        inb = sb("inb", [P, T, K, COLS])
        low = sb("low", [P, K, COLS])
        lin = sb("lin", [P, K, COLS])
        rest = sb("rest", [P, K, COLS])
        s_parts = sb("s_parts", [P, 2, PARTS, K, COLS], BF16)
        negb = sb("negb", [P, K])
        bmr = sb("bmr", [P, NC])
        oma = sb("oma", [P, 1])

        s_half = [sem(f"first_image_loaded{h}") for h in range(2)]
        s_x = [None] + [sem(f"x_loaded{n}") for n in range(1, N)]
        s_gavg = sem("gavg_loaded")
        s_small = sem("small_loaded")
        s_w12 = {l: sem(f"w12_loaded{l}") for l in (0, 2)}
        s_w3 = {l: sem(f"w3_loaded{l}") for l in (0, 2)}
        s_wc = {l: sem(f"wc_loaded{l}") for l in (1, 3)}
        s_rest = {l: sem(f"weight_rest_ready{l}") for l in (1, 3)}
        s_mhalf = sem("mhalf_set")
        s_warm = sem("warmed_up")
        s_zeros = sem("zeros_set")
        s_out = sem("out_stored")

        norm = [NormSems(sem, l) for l in range(4)]
        att = {l: AttentionSems(sem, l) for l in (0, 2)}
        scan = {l: ScanSems(sem, l) for l in (1, 3)}
        s_dve = sem("vector_chain")

        def image_in(l, n):
            if l == 0:
                return x0[:, n]
            return xw.rearrange("p w k (n h) -> p n k h w", n=N)[:, n]

        def image_out(l, n):
            dst = xw if l == 0 else xh
            return dst.rearrange("p t k (n j) -> p n k t j", n=N)[:, n]

        def norm_rounds(l):
            return [(0, K), (K, NC)] if l in (0, 2) else [(0, NC)]

        def images(engine, image):
            image(0, 0, first=True)
            with engine.Fori(0, (N - 2) // 2) as pair:
                image(pair * 2 + 1, 1)
                image(pair * 2 + 2, 0)
            image(N - 1, 1, last=True)

        def o_bank(m):
            return bank[(4, 4, 5, 6)[m]][:, (0, POS, 0, 0)[m]:(POS, 2 * POS, POS, POS)[m]]

        block = ctx.enter_context(nc.Block())

        @block.sync
        def _(sp):
            sp.dma_start(x0[:, 0, 0:K // 2], a["x"][:, 0, 0:K // 2]).then_inc(s_half[0], 16)
            sp.dma_start(gavg[:], a["gavg"]).then_inc(s_gavg, 16)
            sp.dma_start(par[:], a["par"]).then_inc(s_small, 16)
            sp.dma_start(ident[:], a["ident"]).then_inc(s_small, 16)
            sp.dma_start(w3[0][:], a["w3_0"]).then_inc(s_w3[0], 16)
            for n in range(1, N):
                sp.dma_start(x0[:, n], a["x"][:, n]).then_inc(s_x[n], 16)
            sp.dma_start(wc[1][:], a["wc1"]).then_inc(s_wc[1], 16)
            sp.dma_start(w12[2][:], a["w12_2"]).then_inc(s_w12[2], 16)
            sp.dma_start(w3[2][:], a["w3_2"]).then_inc(s_w3[2], 16)
            sp.dma_start(wc[3][:], a["wc3"]).then_inc(s_wc[3], 16)
            with sp.Fori(0, T - 1) as i:
                t = i * -1 + (T - 1)
                sp.wait_ge(scan[3].taken, i + T)
                sp.dma_start(a["out"][:, t], xh[:, t]).then_inc(s_out, 16)
            for u in range(K // PAIR):
                sp.wait_ge(scan[3].result, u + 1)
                ks = slice(u * PAIR, (u + 1) * PAIR)
                sp.dma_start(a["out"][:, 0, ks], xh[:, 0, ks]).then_inc(s_out, 16)
            sp.wait_ge(s_out, 16 * (T - 1 + K // PAIR))

        @block.tensor
        def _(pe):
            def keep_warm(count):
                for _ in range(count):
                    nc.tensor.matmul(bank[7][:], zeros[:, 0:P], zeros[:], start=True, stop=True)

            def group_means(l, r):
                s = norm[l]
                c0, c1 = norm_rounds(l)[r]
                pe.wait_ge(s.stats, c1)
                if l == 0 and r == 0:
                    pe.wait_ge(s_gavg, 16)
                nc.tensor.matmul(bank[4][:, 0:(c1 - c0) * SETS], gavg[:], st[:, c0:c1, :, 1],
                                 start=True, stop=True).then_inc(s.mean, 1)

            def group_variances(l, r):
                s = norm[l]
                c0, c1 = norm_rounds(l)[r]
                pe.wait_ge(s.vadd, r + 1)
                nc.tensor.matmul(bank[5][:, 0:(c1 - c0) * SETS], gavg[:], vadd[:, c0:c1],
                                 start=True, stop=True).then_inc(s.var, 1)

            def attention(l):
                s = att[l]
                pe.wait_ge(s_w12[l], 16)

                def relu_branch(xn_s, m, done):
                    for k in range(K):
                        mm = nc.tensor.matmul(bank[2 + m // 2][:, m % 2 * POS:(m % 2 + 1) * POS],
                                              w3[l][:, k, m * P:(m + 1) * P], xn_s[:, k],
                                              start=(k == 0), stop=(k == K - 1))
                    if done:
                        mm.then_inc(s.a_mm, 1)

                if l == 0:
                    pe.wait_ge(s_small, 32)

                def image(n, h, first=False, last=False):
                    for k in range(K):
                        pe.wait_ge(s.xn_ready, n * K + k + 1)
                        mm = nc.tensor.matmul(bank[1][:, 0:POS], w12[l][:, k], xn[h][:, k],
                                              start=(k == 0), stop=(k == K - 1))
                    mm.then_inc(s.e_mm, 1)
                    if not first:
                        pe.wait_ge(s.x_done, n * K)
                    for pc in range(PC):
                        for k in range(K):
                            mm = nc.tensor.transpose(bank[6 + pc][:, k * P:(k + 1) * P],
                                                     xn[h][:, k, pc * P:(pc + 1) * P], ident[:])
                        mm.then_inc(s.xnT_mm, 1)
                    if first:
                        pe.wait_ge(s_w3[l], 16)
                    relu_branch(xn[h], 0, False)
                    pe.wait_ge(s.e_ready, (n + 1) * 2)
                    for ic in range(PC):
                        mm = nc.tensor.matmul(bank[0][:, ic * POS:(ic + 1) * POS],
                                              e1[:, ic * P:(ic + 1) * P], e2[:], start=True, stop=True)
                    mm.then_inc(s.s_mm, 1)
                    if first:
                        group_means(l, 1)
                    relu_branch(xn[h], 1, True)
                    if first:
                        group_variances(l, 1)
                    relu_branch(xn[h], 2, False)
                    pe.wait_ge(s.p_ready, (n + 1) * PC)
                    for jc in range(PC):
                        for ic in range(PC):
                            mm = nc.tensor.transpose(bank[1 - jc][:, ic * P:(ic + 1) * P],
                                                     prob[:, ic, jc * P:(jc + 1) * P], ident[:])
                        mm.then_inc(s.pt_mm, 1)
                    relu_branch(xn[h], 3, True)
                    pe.wait_ge(s.xnT_copied, (n + 1) * PC)
                    pe.wait_ge(s.pt_copied, (n + 1) * PC)
                    for m in range(K):
                        for jc in range(PC):
                            mm = nc.tensor.matmul(o_bank(m),
                                                  xnT[:, jc, m * P:(m + 1) * P], probT[:, jc],
                                                  start=(jc == 0), stop=(jc == PC - 1))
                        if m:
                            mm.then_inc(s.o_mm, 1)
                        if m == 1:
                            pe.wait_ge(s.r_ready, (n + 1) * K)

                images(pe, image)

            def scan_layer(l):
                s = scan[l]
                pe.wait_ge(s.w, PARTS)

                def step(q, h):
                    seen = set()
                    for j, (u, parts, v) in enumerate(PHASES[l]):
                        first = all(o[2] != v for o in PHASES[l][:j])
                        final = all(o[2] != v for o in PHASES[l][j + 1:])
                        todo = [(k, m, wp, part) for m in range(PAIR) for k in range(u * PAIR, (u + 1) * PAIR)
                                for wp in range(PARTS) for part in parts]
                        for n, (k, m, wp, part) in enumerate(todo):
                            if (u, part) not in seen:
                                pe.wait_ge(s.parts[u], q * PARTS + part + 1)
                                seen.add((u, part))
                            c = v * PAIR + m
                            mm = nc.tensor.matmul(
                                bank[(K // PAIR) * h + v][:, m * COLS:(m + 1) * COLS],
                                w_parts[l][:, wp, k, c * P:(c + 1) * P], s_parts[:, h, part, k],
                                start=first and n == 0, stop=final and n == len(todo) - 1, skip_group_check=True)
                        if final:
                            mm.then_inc(s.y[v], 1)

                with pe.Fori(0, T - 1) as i:
                    for h in range(2):
                        step(i * 2 + h, h)

            def first_norm(l):
                keep_warm(WARM_STATS[l])
                group_means(l, 0)
                keep_warm(WARM_MEANS[l])
                group_variances(l, 0)
                keep_warm(WARM_VARIANCES[l])

            pe.wait_ge(s_zeros, 1)
            for l in range(0, 4, 2):
                first_norm(l)
                attention(l)
                first_norm(l + 1)
                scan_layer(l + 1)

        @block.scalar
        def _(act):
            act.dma_start(x0[:, 0, K // 2:], a["x"][:, 0, K // 2:]).then_inc(s_half[1], 16)
            act.dma_start(w12[0][:], a["w12_0"]).then_inc(s_w12[0], 16)

            def attention(l, b12, b3):
                s = att[l]

                def image(n, h, first=False, last=False):
                    act.wait_ge(s.e_mm, n + 1)
                    nc.scalar.activation(e1[:], bank[1][0:D, 0:POS], ACT.Relu,
                                         bias=par[0:D, b12:b12 + 1]).then_inc(s.e_ready, 1)
                    nc.scalar.activation(e2[:], bank[1][D:2 * D, 0:POS], ACT.Relu,
                                         bias=par[D:2 * D, b12:b12 + 1]).then_inc(s.e_ready, 1)
                    act.wait_ge(s.xnT_mm, n * PC + 1)
                    nc.scalar.copy(xnT[:, 0], bank[6][:]).then_inc(s.xnT_copied, 1)
                    act.wait_ge(s.nmx_ready, n + 1)
                    for ic in range(PC):
                        nc.scalar.activation(prob[:, ic], bank[0][:, ic * POS:(ic + 1) * POS], ACT.Exp,
                                             bias=nmx[:, ic:ic + 1], accum_out=rsum[:, ic:ic + 1])\
                            .then_inc(s.exp_done, 1)
                    def normalise_next():
                        act.wait_ge(norm[l].done, 2)
                        for k in range(K):
                            src, dst = image_in(l, n + 1)[:, k], xn[1 - h][:, k]
                            if l == 2:
                                dst = dst.rearrange("p (t j) -> p t j", t=T)
                            c = (n + 1) * K + k
                            nc.scalar.activation(dst, src, ACT.Identity, bias=nmr[:, bass.ds(c, 1)],
                                                 scale=rstd[:, bass.ds(c, 1)]).then_inc(s.xn_ready, 1)

                    for m in range(K):
                        if m == 0:
                            act.wait_ge(s.a_mm, n * 2 + 1)
                        if m == 2:
                            act.wait_ge(s.pt_mm, n * PC + 1)
                            nc.scalar.copy(probT[:, 0], bank[1][:, 0:POS]).then_inc(s.pt_copied, 1)
                            if not last and not first:
                                normalise_next()
                            act.wait_ge(s.a_mm, n * 2 + 2)
                        nc.scalar.activation(rel[:, m], bank[2 + m // 2][:, m % 2 * POS:(m % 2 + 1) * POS],
                                             ACT.Relu, bias=par[:, b3 + m:b3 + m + 1]).then_inc(s.r_ready, 1)
                    if first:
                        normalise_next()

                images(act, image)

            def scan_inputs(l, xr):
                act.wait_ge(scan[l].bias, 1)
                for n in range(N):
                    for k in range(K):
                        c = n * K + k
                        nc.scalar.activation(inb[:, 2:, k, n * T:(n + 1) * T], xr[:, 2:, k, n * T:(n + 1) * T],
                                             ACT.Identity, bias=bmr[:, c:c + 1], scale=rstd[:, c:c + 1])\
                            .then_inc(scan[l].inb, 1)

            def load_table(i, function):
                if i:
                    act.wait_ge(s_warm, i)
                nc.scalar.activation(warm[:], warm[:] if i else zeros[:, 0:1], function).then_inc(s_warm, 1)

            def root_of_variance(l):
                act.wait_ge(norm[l].gvar, 1)
                nc.scalar.activation(root[:], gvar[:], ACT.Sqrt).then_inc(norm[l].std, 1)

            act.wait_ge(s_zeros, 1)
            load_table(0, ACT.Exp)
            act.wait_ge(s_small, 32)
            attention(0, B12_0, B3_0)
            load_table(1, ACT.Sqrt)
            root_of_variance(1)
            scan_inputs(1, xw)
            load_table(2, ACT.Exp)
            attention(2, B12_2, B3_2)
            load_table(3, ACT.Sqrt)
            root_of_variance(3)
            scan_inputs(3, xh)

        @block.vector
        def _(dve):
            chain = [0]

            def link(ins):
                chain[0] += 1
                ins.then_inc(s_dve, 1)
                dve.wait_ge(s_dve, chain[0])

            def column_stats(l, n, k, src):
                nc.vector.bn_stats(st[:, n * K + k].rearrange("p a b -> p (a b)"), src).then_inc(norm[l].stats, 1)

            def image_stats(l, n):
                for k in range(K):
                    if l == 0:
                        if n == 0 and k % (K // 2) == 0:
                            dve.wait_ge(s_half[k // (K // 2)], 16)
                        column_stats(0, n, k, x0[:, n, k])
                    else:
                        column_stats(2, n, k, xw[:, :, k, n * T:(n + 1) * T])

            def set_variances(l, r):
                s = norm[l]
                c0, c1 = norm_rounds(l)[r]
                dve.wait_ge(s.stats, c1)
                nc.vector.tensor_scalar(svar[:, c0:c1], st[:, c0:c1, :, 2], SETS / POS, EPS, ALU.mult, ALU.add)\
                    .then_inc(s_dve, 1)
                chain[0] += 1
                dve.wait_ge(s.mean, r + 1)
                link(nc.vector.reduce_sum(gmean[:, c0:c1], bank[4][:, 0:(c1 - c0) * SETS]
                                          .rearrange("p (c s) -> p c s", s=SETS), AX_X))
                link(nc.vector.tensor_tensor(dev[:, c0:c1], st[:, c0:c1, :, 1],
                                             gmean[:, c0:c1].unsqueeze(2).to_broadcast([P, c1 - c0, SETS]),
                                             ALU.subtract))
                link(nc.vector.tensor_tensor(dev2[:, c0:c1], dev[:, c0:c1], dev[:, c0:c1], ALU.mult))
                nc.vector.tensor_tensor(vadd[:, c0:c1], svar[:, c0:c1], dev2[:, c0:c1], ALU.add).then_inc(s.vadd, 1)
                nc.vector.tensor_scalar(gneg[:, c0:c1], gmean[:, c0:c1], -1.0, None, ALU.mult).then_inc(s.neg, 1)

            def variances(l, r):
                s = norm[l]
                c0, c1 = norm_rounds(l)[r]
                dve.wait_ge(s.var, r + 1)
                nc.vector.reduce_sum(gvar[:, c0:c1], bank[5][:, 0:(c1 - c0) * SETS]
                                     .rearrange("p (c s) -> p c s", s=SETS), AX_X).then_inc(s.gvar, 1)

            def inverse_std(l):
                s = norm[l]
                dve.wait_ge(s.std, 1)
                link(nc.vector.reciprocal(inv[:], root[:]))
                link(nc.vector.scalar_tensor_tensor(half[:], inv[:], -0.5, gvar[:], ALU.mult, ALU.mult))
                link(nc.vector.tensor_tensor(err[:], half[:], inv[:], ALU.mult))
                nc.vector.scalar_tensor_tensor(rstd[:], err[:], 1.5, inv[:], ALU.add, ALU.mult).then_inc(s.rstd, 1)

            def normalise_first(l):
                dve.wait_ge(norm[l].done, 1)
                for k in range(K):
                    dst = xn[0][:, k]
                    if l == 2:
                        dst = dst.rearrange("p (t j) -> p t j", t=T)
                    nc.vector.tensor_scalar(dst, image_in(l, 0)[:, k], rstd[:, k:k + 1], nmr[:, k:k + 1],
                                            ALU.mult, ALU.add).then_inc(att[l].xn_ready, 1)

            def attention(l, alpha):
                s = att[l]

                def image(n, h, first=False, last=False):
                    dve.wait_ge(s.xnT_mm, n * PC + 2)
                    nc.vector.tensor_copy(xnT[:, 1], bank[7][:]).then_inc(s.xnT_copied, 1)
                    dve.wait_ge(s.s_mm, n + 1)
                    nc.vector.reduce_max(mx[:], bank[0][:].rearrange("p (c j) -> p c j", c=PC), AX_X)\
                        .then_inc(s.chain, 1)
                    dve.wait_ge(s.chain, n * 2 + 1)
                    nc.vector.tensor_scalar(nmx[:], mx[:], -1.0, None, ALU.mult).then_inc(s.nmx_ready, 1)
                    if first:
                        set_variances(l, 1)
                    dve.wait_ge(s.exp_done, (n + 1) * PC)
                    nc.vector.reciprocal(rrec[:], rsum[:]).then_inc(s.chain, 1)
                    dve.wait_ge(s.chain, n * 2 + 2)
                    for ic in range(PC):
                        nc.vector.tensor_scalar(prob[:, ic], prob[:, ic], rrec[:, ic:ic + 1],
                                                par[:, alpha:alpha + 1], ALU.mult, ALU.mult)\
                            .then_inc(s.p_ready, 1)
                    if first:
                        variances(l, 1)

                    def add_residual(m):
                        dve.wait_ge(s.r_ready, n * K + m + 1)
                        dst, r, x = rx[:, m], rel[:, m], image_in(l, n)[:, m]
                        if l == 2:
                            dst, r = (v.rearrange("p (t j) -> p t j", t=T) for v in (dst, r))
                        nc.vector.tensor_tensor(dst, r, x, ALU.add).then_inc(s.rx_done, 1)

                    add_residual(0)
                    add_residual(1)
                    dve.wait_ge(s.pt_mm, n * PC + 2)
                    nc.vector.tensor_copy(probT[:, 1], bank[0][:, 0:POS]).then_inc(s.pt_copied, 1)
                    add_residual(2)
                    add_residual(3)
                    for i, ms in enumerate(((0, 1), (2,), (3,))):
                        dve.wait_ge(s.o_mm, n * 3 + i + 1)
                        for m in ms:
                            dve.wait_ge(s.rx_done, n * K + m + 1)
                            o, r = (v.rearrange("p (t j) -> p t j", t=T)
                                    for v in (o_bank(m), rx[:, m]))
                            nc.vector.tensor_tensor(image_out(l, n)[:, m], o, r, ALU.add).then_inc(s.x_done, 1)
                        for m in ms:
                            dve.wait_ge(s.x_done, n * K + m + 1)
                            column_stats(l + 1, n, m, image_out(l, n)[:, m])

                images(dve, image)

            def scan_layer(l, xr, cb):
                s = scan[l]
                nc.vector.tensor_scalar(negb[:], par[:, cb:cb + K], -1.0, None, ALU.mult).then_inc(s_dve, 1)
                chain[0] += 1

                def wide(v):
                    return v[:].rearrange("p (n k) -> p k n", n=N).unsqueeze(3).to_broadcast([P, K, N, T])

                def strip(v):
                    return v.rearrange("p k (n j) -> p k n j", j=T)

                def wide_pair(v, u):
                    return wide(v)[:, u * PAIR:(u + 1) * PAIR]

                def first_scaled(u, ks):
                    nc.vector.tensor_tensor(strip(rest[:, ks]), strip(xr[:, 0, ks]), wide_pair(rstd, u), ALU.mult)\
                        .then_inc(s.scaled, 1)

                def first_part(u, ks):
                    dve.wait_ge(s.scaled, u + 1)
                    nc.vector.tensor_tensor(strip(s_parts[:, 0, 0, ks]), strip(rest[:, ks]), wide_pair(nmr, u),
                                            ALU.add).then_inc(s.parts[u], 1)

                def first_whole(u, ks):
                    dve.wait_ge(s.scaled, u + 1)
                    nc.vector.tensor_tensor(strip(state[:, 0, ks]), strip(rest[:, ks]), wide_pair(nmr, u), ALU.add)\
                        .then_inc(s.first, 1)

                def first_left(u, ks):
                    dve.wait_ge(s.first, u + 1)
                    nc.vector.tensor_tensor(rest[:, ks], state[:, 0, ks], s_parts[:, 0, 0, ks], ALU.subtract)\
                        .then_inc(s.first_rest, 1)

                def second_part(u, ks):
                    dve.wait_ge(s.first_rest, u + 1)
                    nc.vector.tensor_copy(s_parts[:, 0, 1, ks], rest[:, ks]).then_inc(s.parts[u], 1)

                def third_part(u, ks):
                    dve.wait_ge(s.parts[u], 2)
                    nc.vector.tensor_tensor(s_parts[:, 0, 2, ks], rest[:, ks], s_parts[:, 0, 1, ks], ALU.subtract)\
                        .then_inc(s.parts[u], 1)

                dve.wait_ge(norm[l].rstd, 1)
                nc.vector.tensor_tensor(nmr[:], gneg[:], rstd[:], ALU.mult).then_inc(norm[l].done, 1)
                first_stages = [(first_scaled, 0), (first_scaled, 1), (first_part, 0), (first_whole, 0),
                                (first_part, 1), (first_left, 0), (first_whole, 1), (second_part, 0),
                                (first_left, 1), (third_part, 0), (second_part, 1), (third_part, 1)]
                for i, (stage, u) in enumerate(first_stages):
                    if i == K // PAIR:
                        dve.wait_ge(norm[l].done, 1)
                    stage(u, slice(u * PAIR, (u + 1) * PAIR))
                for u in range(K // PAIR):
                    dve.wait_ge(s.parts[u], PARTS)
                link(nc.vector.tensor_tensor(strip(rest[:]), strip(xr[:, 1]), wide(rstd), ALU.mult))
                dve.wait_ge(s.bias, 1)
                link(nc.vector.tensor_tensor(strip(inb[:, 1]), strip(rest[:]), wide(bmr), ALU.add))

                def chunks(u):
                    return slice(u * PAIR, (u + 1) * PAIR)

                def product(u, h):
                    return bank[(K // PAIR) * h + u][:, 0:PAIR * COLS].rearrange("p (m c) -> p m c", m=PAIR)

                def is_last(q):
                    return isinstance(q, int) and q == 2 * T - 3

                def new_state(q, h):
                    return xr[:, 0] if is_last(q) else state[:, 1 - h]

                def relu_state(q, t, h, u):
                    dve.wait_ge(s.y[u], q + 1)
                    for k in range(u * PAIR, (u + 1) * PAIR):
                        last = nc.vector.scalar_tensor_tensor(
                            new_state(q, h)[:, k], product(u, h)[:, k % PAIR], negb[:, k:k + 1], inb[:, t, k],
                            ALU.max, ALU.add)
                    last.then_inc(s.result if is_last(q) else s.state[u], 1)

                def prelu_low(q, t, h, u):
                    dve.wait_ge(s.y[u], q + 1)
                    nc.vector.tensor_tensor(low[:, chunks(u)], product(u, h),
                                            negb[:, chunks(u)].unsqueeze(2).to_broadcast([P, PAIR, COLS]),
                                            ALU.max).then_inc(s.terms[u], 1)

                def prelu_lin(q, t, h, u):
                    nc.vector.scalar_tensor_tensor(lin[:, chunks(u)], product(u, h), par[:, PA_1:PA_1 + 1],
                                                   inb[:, t, chunks(u)], ALU.mult, ALU.add)\
                        .then_inc(s.terms[u], 1)

                def prelu_state(q, t, h, u):
                    dve.wait_ge(s.terms[u], q * 2 + 2)
                    nc.vector.scalar_tensor_tensor(new_state(q, h)[:, chunks(u)], low[:, chunks(u)], oma[:, 0:1],
                                                   lin[:, chunks(u)], ALU.mult, ALU.add)\
                        .then_inc(s.result if is_last(q) else s.state[u], 1)

                def prelu_first_part(q, t, h, u):
                    dve.wait_ge(s.terms[u], q * 2 + 2)
                    nc.vector.scalar_tensor_tensor(s_parts[:, 1 - h, 0, chunks(u)], low[:, chunks(u)], oma[:, 0:1],
                                                   lin[:, chunks(u)], ALU.mult, ALU.add).then_inc(s.parts[u], 1)

                def split_first(q, t, h, u):
                    dve.wait_ge(s.state[u], q + 1)
                    nc.vector.tensor_copy(s_parts[:, 1 - h, 0, chunks(u)], state[:, 1 - h, chunks(u)])\
                        .then_inc(s.parts[u], 1)

                def split_rest(q, t, h, u):
                    if l == 1 and u == 0:
                        dve.wait_ge(s.state[u], q + 1)
                    else:
                        dve.wait_ge(s.parts[u], (q + 1) * PARTS + 1)
                    nc.vector.tensor_tensor(rest[:, chunks(u)], state[:, 1 - h, chunks(u)],
                                            s_parts[:, 1 - h, 0, chunks(u)], ALU.subtract).then_inc(s.rest[u], 1)

                def split_second(q, t, h, u):
                    dve.wait_ge(s.rest[u], q + 1)
                    nc.vector.tensor_copy(s_parts[:, 1 - h, 1, chunks(u)], rest[:, chunks(u)])\
                        .then_inc(s.parts[u], 1)

                def split_third(q, t, h, u):
                    dve.wait_ge(s.parts[u], (q + 1) * PARTS + 2)
                    nc.vector.tensor_tensor(s_parts[:, 1 - h, 2, chunks(u)], rest[:, chunks(u)],
                                            s_parts[:, 1 - h, 1, chunks(u)], ALU.subtract).then_inc(s.parts[u], 1)

                def third_of_lower(q, t, h, u):
                    dve.wait_ge(s.parts[u], (q + 1) * PARTS + 2)
                    nc.vector.tensor_tensor(s_parts[:, 1 - h, 2, u * PAIR], rest[:, u * PAIR],
                                            s_parts[:, 1 - h, 1, u * PAIR], ALU.subtract)

                def third_of_upper(q, t, h, u):
                    k = u * PAIR + 1
                    nc.vector.tensor_tensor(s_parts[:, 1 - h, 2, k], rest[:, k],
                                            s_parts[:, 1 - h, 1, k], ALU.subtract).then_inc(s.parts[u], 1)

                stages = {
                    1: [(prelu_low, 0), (prelu_lin, 0), (prelu_first_part, 0), (prelu_state, 0), (split_rest, 0),
                        (prelu_low, 1), (split_second, 0), (prelu_lin, 1), (third_of_lower, 0),
                        (prelu_state, 1), (third_of_upper, 0), (split_first, 1), (split_rest, 1),
                        (split_second, 1), (split_third, 1)],
                    3: [(stage, u) for u in range(K // PAIR)
                        for stage in (relu_state, split_first, split_rest, split_second, split_third)]}[l]

                def step(q, t, h):
                    if not (isinstance(q, int) and q == 0):
                        dve.wait_ge(s.taken, q)
                    if is_last(q):
                        dve.wait_ge(s.last_in, 1)
                    for stage, u in stages:
                        if not is_last(q) or stage in (relu_state, prelu_low, prelu_lin, prelu_state):
                            stage(q, t, h, u)

                step(0, 1, 0)
                dve.wait_ge(s.inb, NC)
                with dve.Fori(0, (T - 2) // 2) as i:
                    for h in range(2):
                        step(i * 2 + 1 + h, i * 2 + 2 + h, 1 - h)
                dve.wait_ge(s.taken, T - 1)
                step(T - 1, T - 2, 1)
                with dve.Fori(0, (T - 4) // 2) as i:
                    last = i * -2 + (T - 3)
                    for h in range(2):
                        step(i * 2 + T + h, last + -h, h)
                step(2 * T - 4, 1, 0)
                step(2 * T - 3, 0, 1)

            def first_image(l):
                def stats(n):
                    if l == 0 and n:
                        dve.wait_ge(s_x[n], 16)
                    image_stats(l, n)

                stats(0)
                set_variances(l, 0)
                variances(l, 0)
                if l == 2:
                    stats(1)
                normalise_first(l)
                for n in range(1 if l == 0 else 2, N):
                    stats(n)

            nc.vector.memset(zeros[:], 0.0).then_inc(s_zeros, 1)
            nc.vector.memset(mhalf[:], -0.5).then_inc(s_mhalf, 1)
            first_image(0)
            dve.wait_ge(s_small, 32)
            nc.vector.tensor_scalar(oma[:], par[:, PA_1:PA_1 + 1], -1.0, 1.0, ALU.mult, ALU.add)\
                .then_inc(s_mhalf, 1)
            attention(0, AL_0)
            set_variances(1, 0)
            variances(1, 0)
            inverse_std(1)
            scan_layer(1, xw, CB_1)
            dve.wait_ge(scan[1].taken, 2 * T - 2)
            dve.wait_ge(scan[1].result, K // PAIR)
            first_image(2)
            attention(2, AL_2)
            set_variances(3, 0)
            variances(3, 0)
            inverse_std(3)
            scan_layer(3, xh, CB_3)

        @block.gpsimd
        def _(pool):
            def inverse_std(l):
                s = norm[l]
                for r, (c0, c1) in enumerate(norm_rounds(l)):
                    pool.wait_ge(s.gvar, r + 1)
                    nc.gpsimd.tensor_tensor(rstd[:, c0:c1], gvar[:, c0:c1], mhalf[:, c0:c1], ALU.pow)\
                        .then_inc(s.rstd, 1)
                    pool.wait_ge(s.neg, r + 1)
                    pool.wait_ge(s.rstd, r + 1)
                    nc.gpsimd.tensor_tensor(nmr[:, c0:c1], gneg[:, c0:c1], rstd[:, c0:c1], ALU.mult)\
                        .then_inc(s.done, 1)

            def split_weights(l):
                s = scan[l]
                pool.wait_ge(s_wc[l], 16)
                w = wc[l]
                nc.gpsimd.tensor_copy(w_parts[l][:, 0], w[:]).then_inc(s.w, 1)
                pool.wait_ge(s.w, 1)
                nc.gpsimd.tensor_tensor(w[:], w[:], w_parts[l][:, 0], ALU.subtract).then_inc(s_rest[l], 1)
                pool.wait_ge(s_rest[l], 1)
                nc.gpsimd.tensor_copy(w_parts[l][:, 1], w[:]).then_inc(s.w, 1)
                pool.wait_ge(s.w, 2)
                nc.gpsimd.tensor_tensor(w_parts[l][:, 2], w[:], w_parts[l][:, 1], ALU.subtract).then_inc(s.w, 1)

            def scan_layer(l, xr, cb):
                s = scan[l]
                pairs = range(K // PAIR)
                bias = par[:, cb:cb + K].unsqueeze(2).to_broadcast([P, K, COLS])

                pool.wait_ge(norm[l].done, 1)
                nc.gpsimd.tensor_tensor(bmr[:].rearrange("p (n k) -> p k n", n=N),
                                        nmr[:].rearrange("p (n k) -> p k n", n=N),
                                        par[:, cb:cb + K].unsqueeze(2).to_broadcast([P, K, N]), ALU.add)\
                    .then_inc(s.bias, 1)
                pool.wait_ge(s.first, K // PAIR)
                nc.gpsimd.tensor_tensor(inb[:, 0], state[:, 0], bias, ALU.add).then_inc(s.taken, 1)
                pool.wait_ge(s.taken, 1)
                nc.gpsimd.tensor_tensor(inb[:, 0], inb[:, 0], xr[:, 0], ALU.add).then_inc(s.last_in, 1)
                with pool.Fori(0, (T - 2) // 2) as i:
                    for h in range(2):
                        t = i * 2 + 1 + h
                        for u in pairs:
                            pool.wait_ge(s.state[u], t)
                        nc.gpsimd.tensor_tensor(inb[:, t], state[:, 1 - h], bias, ALU.add).then_inc(s.taken, 1)

                def add_state(j, t, h):
                    for u in pairs:
                        pool.wait_ge(s.state[u], j)
                    nc.gpsimd.tensor_tensor(xr[:, t], xr[:, t], state[:, h], ALU.add).then_inc(s.taken, 1)

                add_state(T - 1, T - 1, 1)
                with pool.Fori(0, (T - 2) // 2) as i:
                    last = i * -2 + (T - 2)
                    for h in range(2):
                        add_state(i * 2 + T + h, last + -h, h)

            pool.wait_ge(s_mhalf, 1)
            inverse_std(0)
            split_weights(1)
            scan_layer(1, xw, CB_1)
            inverse_std(2)
            split_weights(3)
            scan_layer(3, xh, CB_3)


def kernel(**inputs):
    import numpy as np
    import concourse.bacc as bacc
    from concourse.bass_utils import run_bass_kernel_spmd

    def col(v):
        return np.asarray(v).reshape(K, P).T

    def weight(w):
        w = np.asarray(w)
        return np.ascontiguousarray(w.T.reshape(K, P, w.shape[0]).transpose(1, 0, 2))

    def whole(v):
        return np.repeat(np.asarray(v).reshape(1, 1), P, axis=0)

    i = {k: np.asarray(v) for k, v in inputs.items()}
    par = np.concatenate(
        [np.concatenate([i["L0_conv_b1"], i["L0_conv_b2"]])[:, None], col(i["L0_conv_b3"]), whole(i["L0_conv_alpha"]),
         col(i["L1_conv_conv_b"]), whole(i["L1_conv_prelu_a"]),
         np.concatenate([i["L2_conv_b1"], i["L2_conv_b2"]])[:, None], col(i["L2_conv_b3"]), whole(i["L2_conv_alpha"]),
         col(i["L3_conv_b"])], axis=1)
    group = np.arange(P) // CG
    arrays = {
        "x": np.ascontiguousarray(i["x"].reshape(N, K, P, T, T).transpose(2, 0, 1, 4, 3)).reshape(P, N, K, POS),
        "par": np.ascontiguousarray(par),
        "gavg": ((group[:, None] == group[None, :]) / (SETS * CG)).astype(np.float32),
        "ident": np.eye(P, dtype=np.float32),
        "w12_0": weight(np.concatenate([i["L0_conv_w1"], i["L0_conv_w2"]])),
        "w12_2": weight(np.concatenate([i["L2_conv_w1"], i["L2_conv_w2"]])),
        "w3_0": weight(i["L0_conv_w3"]),
        "w3_2": weight(i["L2_conv_w3"]),
        "wc1": weight(i["L1_conv_conv_w"][:, :, 0, i["L1_conv_conv_w"].shape[3] // 2]),
        "wc3": weight(i["L3_conv_W"][:, :, (i["L3_conv_W"].shape[2] - 1) // 2, 0]),
    }
    nc = bacc.Bacc("TRN2", target_bir_lowering=False, num_devices=1)
    aps = {k: nc.dram_tensor(f"in_{k}", v.shape, mybir.dt.from_np(v.dtype), kind="ExternalInput").ap()
           for k, v in arrays.items()}
    aps["out"] = nc.dram_tensor("result", (P, T, K, COLS), F32, kind="ExternalOutput").ap()
    preact_stack(nc, aps)
    r = run_bass_kernel_spmd(nc, [{f"in_{k}": v for k, v in arrays.items()}], core_ids=[0])
    out = r.results[0]["result"].reshape(P, T, K, N, T)
    return np.ascontiguousarray(out.transpose(3, 2, 0, 1, 4)).reshape(N, C, T, T)
```
